# Optimizing a Trainium2 kernel written in Bass

```python
import numpy as np
import jax
import jax.numpy as jnp

def _softmax(x, axis=-1):
    return jax.nn.softmax(x, axis=axis)

def _gelu(x):
    return jax.nn.gelu(x, approximate=True)

def _silu(x):
    return jax.nn.silu(x)

def _sigmoid(x):
    return jax.nn.sigmoid(x)

def _layernorm(x, axis=-1, eps=1e-05):
    m = jnp.mean(x, axis=axis, keepdims=True)
    v = jnp.var(x, axis=axis, keepdims=True)
    return (x - m) / jnp.sqrt(v + eps)

def _scatter_add(tgt, idx, src, axis=0):
    return tgt.at[idx].add(src)

def _segment_sum(src, seg, n):
    return jax.ops.segment_sum(src, seg, n)
kernel_name = 'mk_conv_preact_d4_conv_nhwc256_r4_734199'

def setup_inputs(seed: int=0):
    np.random.seed(seed)
    _w = jnp.asarray

    def _rec_inputs():
        import jax
        import jax.numpy as jnp
        _gk = jax.random.key(seed)
        x = -0.000125 + 0.9999 * jax.random.normal(jax.random.fold_in(_gk, 1), (8, 32, 32, 64), jnp.float32)
        return x
    x = _rec_inputs()

    def _L0_conv_setup():
        import jax, jax.numpy as jnp
        import numpy as np
        B, H, W, C = (8, 32, 32, 64)
        K, DT, EPS = (5, 0.2, 0.001)
        LAM2 = 4.0

        def _dwconv(x, w):
            k = w.reshape(3, 3, 1, C)
            return jax.lax.conv_general_dilated(x, k, (1, 1), 'SAME', dimension_numbers=('NHWC', 'HWIO', 'NHWC'), feature_group_count=C)

        def _bn(x, gamma, beta, mean, var):
            return (x - mean) * jax.lax.rsqrt(var + EPS) * gamma + beta

        def _sobel(x):
            xp = jnp.pad(x, ((0, 0), (1, 1), (1, 1), (0, 0)), mode='reflect')
            top, mid, bot = (xp[:, :-2], xp[:, 1:-1], xp[:, 2:])
            gy = bot[:, :, :-2] + 2 * bot[:, :, 1:-1] + bot[:, :, 2:] - (top[:, :, :-2] + 2 * top[:, :, 1:-1] + top[:, :, 2:])
            gx = top[:, :, 2:] + 2 * mid[:, :, 2:] + bot[:, :, 2:] - (top[:, :, :-2] + 2 * mid[:, :, :-2] + bot[:, :, :-2])
            return (gy, gx)
        key = jax.random.key(seed)
        ks = jax.random.split(key, 6)
        f = jnp.float32
        d = {}
        d['s0'] = jax.random.normal(ks[0], (B, H, W, C), f)
        d['wg'] = jax.random.normal(ks[1], (3, 3, C), f) * 0.1
        d['wg1'] = jax.random.normal(ks[2], (3, 3, C), f) * 0.1
        for i, p in enumerate(['g', 'g1', 'out']):
            k4 = jax.random.split(ks[3 + i], 4)
            d[p + '_gamma'] = 1.0 + 0.1 * jax.random.normal(k4[0], (C,), f)
            d[p + '_beta'] = 0.1 * jax.random.normal(k4[1], (C,), f)
            d[p + '_mean'] = 0.1 * jax.random.normal(k4[2], (C,), f)
            d[p + '_var'] = 0.5 + jax.random.uniform(k4[3], (C,), f)
        return d
    _L0_conv_all = _L0_conv_setup()
    _L0_conv_in = {k: v for k, v in _L0_conv_all.items() if k in ('wg', 'wg1', 'g_gamma', 'g_beta', 'g_mean', 'g_var', 'g1_gamma', 'g1_beta', 'g1_mean', 'g1_var', 'out_gamma', 'out_beta', 'out_mean', 'out_var')}
    del _L0_conv_all

    def _L1_conv_setup():
        import jax, jax.numpy as jnp
        import numpy as np
        from jax import lax
        B, H, W, C_IN, C_OUT = (32, 56, 56, 64, 64)
        KH, KW = (3, 3)
        key = jax.random.key(seed)
        k_in, k_kern, k_bias = jax.random.split(key, 3)
        inputs = jax.random.normal(k_in, (B, H, W, C_IN), dtype=jnp.float32)
        fan_in = KH * KW * C_IN
        kernel = jax.random.normal(k_kern, (KH, KW, C_IN, C_OUT), dtype=jnp.float32) / jnp.sqrt(fan_in).astype(jnp.float32)
        bias = jnp.zeros((C_OUT,), dtype=jnp.float32)
        return {'inputs': inputs, 'kernel': kernel, 'bias': bias}
    _L1_conv_all = _L1_conv_setup()
    _L1_conv_in = {k: v for k, v in _L1_conv_all.items() if k in ('kernel', 'bias')}
    del _L1_conv_all

    def _L2_conv_setup():
        import jax, jax.numpy as jnp
        import numpy as np
        from jax import lax

        def layer_norm(x, g, b, eps=1e-05):
            mu = jnp.mean(x, axis=-1, keepdims=True)
            var = jnp.var(x, axis=-1, keepdims=True)
            return (x - mu) / jnp.sqrt(var + eps) * g + b

        def selective_scan(u, delta, A, Bm, Cm, D):
            Bsz, L, d_inner = u.shape
            N = A.shape[1]

            def step(h, inp):
                u_t, d_t, B_t, C_t = inp
                dA = jnp.exp(d_t[..., None] * A)
                h = dA * h + (d_t * u_t)[..., None] * B_t[:, None, :]
                y = jnp.einsum('bdn,bn->bd', h, C_t)
                return (h, y)
            h0 = jnp.zeros((Bsz, d_inner, N), dtype=u.dtype)
            xs = (u.transpose(1, 0, 2), delta.transpose(1, 0, 2), Bm.transpose(1, 0, 2), Cm.transpose(1, 0, 2))
            _, ys = lax.scan(step, h0, xs)
            return ys.transpose(1, 0, 2) + u * D

        def mamba_block(x, in_proj_w, conv_w, conv_b, x_proj_w, dt_proj_w, dt_proj_b, A_log, D, out_proj_w):
            d_inner = in_proj_w.shape[0] // 2
            d_state = A_log.shape[1]
            dt_rank = dt_proj_w.shape[1]
            d_conv = conv_w.shape[-1]
            xz = x @ in_proj_w.T
            xi, z = jnp.split(xz, 2, axis=-1)
            xt = xi.transpose(0, 2, 1)
            kernel = conv_w[:, None, :]
            xc = lax.conv_general_dilated(xt, kernel, (1,), [(d_conv - 1, 0)], feature_group_count=d_inner, dimension_numbers=('NCH', 'OIH', 'NCH'))
            xc = xc + conv_b[None, :, None]
            xs = jax.nn.silu(xc).transpose(0, 2, 1)
            x_dbl = xs @ x_proj_w.T
            dt, Bm, Cm = jnp.split(x_dbl, [dt_rank, dt_rank + d_state], axis=-1)
            delta = jax.nn.softplus(dt @ dt_proj_w.T + dt_proj_b)
            A = -jnp.exp(A_log)
            y = selective_scan(xs, delta, A, Bm, Cm, D)
            y = y * jax.nn.silu(z)
            return y @ out_proj_w.T
        key = jax.random.key(seed)
        ks = jax.random.split(key, 12)
        B, H, W, C = (4, 32, 32, 64)
        d_state, d_conv, expand = (16, 4, 2)
        d_inner = expand * C
        dt_rank = int(np.ceil(C / 16))
        s = 0.02
        A = jnp.tile(jnp.arange(1, d_state + 1, dtype=jnp.float32)[None, :], (d_inner, 1))
        dt0 = jax.random.uniform(ks[9], (d_inner,), minval=0.001, maxval=0.1)
        return {'x': jax.random.normal(ks[0], (B, H, W, C), jnp.float32), 'ln_g': jnp.ones((C,), jnp.float32), 'ln_b': jnp.zeros((C,), jnp.float32), 'in_proj_w': jax.random.normal(ks[1], (2 * d_inner, C), jnp.float32) * s, 'conv_w': jax.random.normal(ks[2], (d_inner, d_conv), jnp.float32) * s, 'conv_b': jnp.zeros((d_inner,), jnp.float32), 'x_proj_w': jax.random.normal(ks[3], (dt_rank + 2 * d_state, d_inner), jnp.float32) * s, 'dt_proj_w': jax.random.normal(ks[4], (d_inner, dt_rank), jnp.float32) * dt_rank ** (-0.5), 'dt_proj_b': jnp.log(jnp.expm1(dt0)), 'A_log': jnp.log(A), 'D': jnp.ones((d_inner,), jnp.float32), 'out_proj_w': jax.random.normal(ks[5], (C, d_inner), jnp.float32) * s, 'proj_w': jax.random.normal(ks[6], (C, C), jnp.float32) * s, 'proj_b': jnp.zeros((C,), jnp.float32), 'skip_scale': jnp.ones((1,), jnp.float32)}
    _L2_conv_all = _L2_conv_setup()
    _L2_conv_in = {k: v for k, v in _L2_conv_all.items() if k in ('ln_g', 'ln_b', 'in_proj_w', 'conv_w', 'conv_b', 'x_proj_w', 'dt_proj_w', 'dt_proj_b', 'A_log', 'D', 'out_proj_w', 'proj_w', 'proj_b', 'skip_scale')}
    del _L2_conv_all

    def _L3_conv_setup():
        import jax, jax.numpy as jnp
        import numpy as np

        def dct2_ortho_matrix(N):
            n = jnp.arange(N, dtype=jnp.float32)
            k = n[:, None]
            M = jnp.cos(jnp.pi * (n[None, :] + 0.5) * k / N) * jnp.sqrt(2.0 / N)
            M = M.at[0].multiply(1.0 / jnp.sqrt(2.0))
            return M
        key = jax.random.key(seed)
        x = jax.random.normal(key, (16, 32, 32, 64), dtype=jnp.float32)
        return {'x': x}
    _L3_conv_all = _L3_conv_setup()
    _L3_conv_in = {k: v for k, v in _L3_conv_all.items() if k in ()}
    del _L3_conv_all
    return {'x': x, 'L0_conv_wg': _L0_conv_in['wg'], 'L0_conv_wg1': _L0_conv_in['wg1'], 'L0_conv_g_gamma': _L0_conv_in['g_gamma'], 'L0_conv_g_beta': _L0_conv_in['g_beta'], 'L0_conv_g_mean': _L0_conv_in['g_mean'], 'L0_conv_g_var': _L0_conv_in['g_var'], 'L0_conv_g1_gamma': _L0_conv_in['g1_gamma'], 'L0_conv_g1_beta': _L0_conv_in['g1_beta'], 'L0_conv_g1_mean': _L0_conv_in['g1_mean'], 'L0_conv_g1_var': _L0_conv_in['g1_var'], 'L0_conv_out_gamma': _L0_conv_in['out_gamma'], 'L0_conv_out_beta': _L0_conv_in['out_beta'], 'L0_conv_out_mean': _L0_conv_in['out_mean'], 'L0_conv_out_var': _L0_conv_in['out_var'], 'L1_conv_kernel': _L1_conv_in['kernel'], 'L1_conv_bias': _L1_conv_in['bias'], 'L2_conv_ln_g': _L2_conv_in['ln_g'], 'L2_conv_ln_b': _L2_conv_in['ln_b'], 'L2_conv_in_proj_w': _L2_conv_in['in_proj_w'], 'L2_conv_conv_w': _L2_conv_in['conv_w'], 'L2_conv_conv_b': _L2_conv_in['conv_b'], 'L2_conv_x_proj_w': _L2_conv_in['x_proj_w'], 'L2_conv_dt_proj_w': _L2_conv_in['dt_proj_w'], 'L2_conv_dt_proj_b': _L2_conv_in['dt_proj_b'], 'L2_conv_A_log': _L2_conv_in['A_log'], 'L2_conv_D': _L2_conv_in['D'], 'L2_conv_out_proj_w': _L2_conv_in['out_proj_w'], 'L2_conv_proj_w': _L2_conv_in['proj_w'], 'L2_conv_proj_b': _L2_conv_in['proj_b'], 'L2_conv_skip_scale': _L2_conv_in['skip_scale']}

def reference(x, L0_conv_wg, L0_conv_wg1, L0_conv_g_gamma, L0_conv_g_beta, L0_conv_g_mean, L0_conv_g_var, L0_conv_g1_gamma, L0_conv_g1_beta, L0_conv_g1_mean, L0_conv_g1_var, L0_conv_out_gamma, L0_conv_out_beta, L0_conv_out_mean, L0_conv_out_var, L1_conv_kernel, L1_conv_bias, L2_conv_ln_g, L2_conv_ln_b, L2_conv_in_proj_w, L2_conv_conv_w, L2_conv_conv_b, L2_conv_x_proj_w, L2_conv_dt_proj_w, L2_conv_dt_proj_b, L2_conv_A_log, L2_conv_D, L2_conv_out_proj_w, L2_conv_proj_w, L2_conv_proj_b, L2_conv_skip_scale):
    import jax
    import jax.numpy as jnp

    def _L0_conv_ref(s0, wg, wg1, g_gamma, g_beta, g_mean, g_var, g1_gamma, g1_beta, g1_mean, g1_var, out_gamma, out_beta, out_mean, out_var):
        import jax, jax.numpy as jnp
        import numpy as np
        B, H, W, C = (8, 32, 32, 64)
        K, DT, EPS = (5, 0.2, 0.001)
        LAM2 = 4.0

        def _dwconv(x, w):
            k = w.reshape(3, 3, 1, C)
            return jax.lax.conv_general_dilated(x, k, (1, 1), 'SAME', dimension_numbers=('NHWC', 'HWIO', 'NHWC'), feature_group_count=C)

        def _bn(x, gamma, beta, mean, var):
            return (x - mean) * jax.lax.rsqrt(var + EPS) * gamma + beta

        def _sobel(x):
            xp = jnp.pad(x, ((0, 0), (1, 1), (1, 1), (0, 0)), mode='reflect')
            top, mid, bot = (xp[:, :-2], xp[:, 1:-1], xp[:, 2:])
            gy = bot[:, :, :-2] + 2 * bot[:, :, 1:-1] + bot[:, :, 2:] - (top[:, :, :-2] + 2 * top[:, :, 1:-1] + top[:, :, 2:])
            gx = top[:, :, 2:] + 2 * mid[:, :, 2:] + bot[:, :, 2:] - (top[:, :, :-2] + 2 * mid[:, :, :-2] + bot[:, :, :-2])
            return (gy, gx)
        fsrc = s0
        h = s0
        h0 = fsrc
        g = jax.nn.relu(_bn(_dwconv(h, wg), g_gamma, g_beta, g_mean, g_var))
        g1 = jax.nn.relu(_bn(_dwconv(h, wg1), g1_gamma, g1_beta, g1_mean, g1_var))
        gy, gx = _sobel(h)
        Dx = 1.0 / (gy * gy / LAM2 + 1.0)
        Dy = 1.0 / (gx * gx / LAM2 + 1.0)
        ux = 0.5 * (jnp.roll(g, 1, axis=2) - jnp.roll(g, -1, axis=2))
        vy = 0.5 * (jnp.roll(g1, 1, axis=3) - jnp.roll(g1, -1, axis=3))
        Ax, Ay = (g * DT, g1 * DT)
        Bx, By = (Dx * DT, Dy * DT)
        E = (ux + vy) * DT
        D = 1.0 / (1.0 + 2.0 * Bx + 2.0 * By)
        cm_x, cp_x = (-Ax + 2.0 * Bx, Ax + 2.0 * Bx)
        cm_y, cp_y = (-Ay + 2.0 * By, Ay + 2.0 * By)
        c0 = 1.0 - 2.0 * Bx - 2.0 * By
        for _ in range(K):
            prev = h
            h = D * (c0 * h0 - 2.0 * E * h + cm_x * jnp.roll(h, 1, axis=2) + cp_x * jnp.roll(h, -1, axis=2) + cm_y * jnp.roll(h, 1, axis=3) + cp_y * jnp.roll(h, -1, axis=3))
            h = h + D * (2.0 * DT) * fsrc
            h0 = prev
        return jax.nn.relu(_bn(h, out_gamma, out_beta, out_mean, out_var))

    def _L1_conv_ref(inputs, kernel, bias):
        import jax, jax.numpy as jnp
        import numpy as np
        from jax import lax
        B, H, W, C_IN, C_OUT = (32, 56, 56, 64, 64)
        KH, KW = (3, 3)
        y = lax.conv_general_dilated(inputs, kernel, window_strides=(1, 1), padding='SAME', lhs_dilation=(1, 1), rhs_dilation=(1, 1), dimension_numbers=('NHWC', 'HWIO', 'NHWC'), feature_group_count=1)
        return y + bias

    def _L2_conv_ref(x, ln_g, ln_b, in_proj_w, conv_w, conv_b, x_proj_w, dt_proj_w, dt_proj_b, A_log, D, out_proj_w, proj_w, proj_b, skip_scale):
        import jax, jax.numpy as jnp
        import numpy as np
        from jax import lax

        def layer_norm(x, g, b, eps=1e-05):
            mu = jnp.mean(x, axis=-1, keepdims=True)
            var = jnp.var(x, axis=-1, keepdims=True)
            return (x - mu) / jnp.sqrt(var + eps) * g + b

        def selective_scan(u, delta, A, Bm, Cm, D):
            Bsz, L, d_inner = u.shape
            N = A.shape[1]

            def step(h, inp):
                u_t, d_t, B_t, C_t = inp
                dA = jnp.exp(d_t[..., None] * A)
                h = dA * h + (d_t * u_t)[..., None] * B_t[:, None, :]
                y = jnp.einsum('bdn,bn->bd', h, C_t)
                return (h, y)
            h0 = jnp.zeros((Bsz, d_inner, N), dtype=u.dtype)
            xs = (u.transpose(1, 0, 2), delta.transpose(1, 0, 2), Bm.transpose(1, 0, 2), Cm.transpose(1, 0, 2))
            _, ys = lax.scan(step, h0, xs)
            return ys.transpose(1, 0, 2) + u * D

        def mamba_block(x, in_proj_w, conv_w, conv_b, x_proj_w, dt_proj_w, dt_proj_b, A_log, D, out_proj_w):
            d_inner = in_proj_w.shape[0] // 2
            d_state = A_log.shape[1]
            dt_rank = dt_proj_w.shape[1]
            d_conv = conv_w.shape[-1]
            xz = x @ in_proj_w.T
            xi, z = jnp.split(xz, 2, axis=-1)
            xt = xi.transpose(0, 2, 1)
            kernel = conv_w[:, None, :]
            xc = lax.conv_general_dilated(xt, kernel, (1,), [(d_conv - 1, 0)], feature_group_count=d_inner, dimension_numbers=('NCH', 'OIH', 'NCH'))
            xc = xc + conv_b[None, :, None]
            xs = jax.nn.silu(xc).transpose(0, 2, 1)
            x_dbl = xs @ x_proj_w.T
            dt, Bm, Cm = jnp.split(x_dbl, [dt_rank, dt_rank + d_state], axis=-1)
            delta = jax.nn.softplus(dt @ dt_proj_w.T + dt_proj_b)
            A = -jnp.exp(A_log)
            y = selective_scan(xs, delta, A, Bm, Cm, D)
            y = y * jax.nn.silu(z)
            return y @ out_proj_w.T
        B, H, W, C = x.shape
        xc = x.transpose(0, 3, 1, 2)
        L = H * W
        x_flat = xc.reshape(B, C, L).transpose(0, 2, 1)
        x_norm = layer_norm(x_flat, ln_g, ln_b)
        y = mamba_block(x_norm, in_proj_w, conv_w, conv_b, x_proj_w, dt_proj_w, dt_proj_b, A_log, D, out_proj_w)
        y = y + skip_scale * x_norm
        y = layer_norm(y, ln_g, ln_b)
        y = y @ proj_w.T + proj_b
        out = y.transpose(0, 2, 1).reshape(B, -1, H, W)
        return out.transpose(0, 2, 3, 1)

    def _L3_conv_ref(x):
        import jax, jax.numpy as jnp
        import numpy as np

        def dct2_ortho_matrix(N):
            n = jnp.arange(N, dtype=jnp.float32)
            k = n[:, None]
            M = jnp.cos(jnp.pi * (n[None, :] + 0.5) * k / N) * jnp.sqrt(2.0 / N)
            M = M.at[0].multiply(1.0 / jnp.sqrt(2.0))
            return M
        B, H, W, C = x.shape
        Mh = dct2_ortho_matrix(H)
        Mw = dct2_ortho_matrix(W)
        y = jnp.einsum('kh,bhwc->bkwc', Mh, x)
        y = jnp.einsum('lw,bkwc->bklc', Mw, y)
        return jnp.transpose(y, (0, 2, 1, 3))

    def _gn(v, G=32, eps=1e-05):
        B_, H_, W_, C_ = v.shape
        g = v.reshape(B_, H_, W_, G, C_ // G)
        m = jnp.mean(g, axis=(1, 2, 4), keepdims=True)
        s = jnp.var(g, axis=(1, 2, 4), keepdims=True)
        return ((g - m) / jnp.sqrt(s + eps)).reshape(v.shape)

    def _ln_c(v, eps=1e-06):
        m = jnp.mean(v, axis=-1, keepdims=True)
        s = jnp.var(v, axis=-1, keepdims=True)
        return (v - m) / jnp.sqrt(s + eps)

    def _ln_t(v, eps=1e-05):
        m = jnp.mean(v, axis=-1, keepdims=True)
        s = jnp.var(v, axis=-1, keepdims=True)
        return (v - m) / jnp.sqrt(s + eps)

    def _to_tokens(v):
        B_, H_, W_, C_ = v.shape
        return v.reshape(B_, H_ * W_, C_)

    def _from_tokens(t, like):
        return t.reshape(like.shape)
    x = x + _L0_conv_ref(_gn(x), L0_conv_wg, L0_conv_wg1, L0_conv_g_gamma, L0_conv_g_beta, L0_conv_g_mean, L0_conv_g_var, L0_conv_g1_gamma, L0_conv_g1_beta, L0_conv_g1_mean, L0_conv_g1_var, L0_conv_out_gamma, L0_conv_out_beta, L0_conv_out_mean, L0_conv_out_var)
    x = x + _L1_conv_ref(_gn(x), L1_conv_kernel, L1_conv_bias)
    x = x + _L2_conv_ref(_gn(x), L2_conv_ln_g, L2_conv_ln_b, L2_conv_in_proj_w, L2_conv_conv_w, L2_conv_conv_b, L2_conv_x_proj_w, L2_conv_dt_proj_w, L2_conv_dt_proj_b, L2_conv_A_log, L2_conv_D, L2_conv_out_proj_w, L2_conv_proj_w, L2_conv_proj_b, L2_conv_skip_scale)
    x = x + _L3_conv_ref(_gn(x))
    return x

_drawn_inputs = setup_inputs


def setup_inputs(seed=0):
    import zlib

    import numpy as np

    out = dict(_drawn_inputs(seed))
    spreads = {'L1_conv_bias': (0.0, 0.1),
     'L2_conv_ln_g': (1.0, 0.2),
     'L2_conv_ln_b': (0.0, 0.517),
     'L2_conv_conv_b': (0.0, 0.8),
     'L2_conv_D': (1.0, 0.6),
     'L2_conv_proj_b': (0.0, 0.1)}
    factors = {'L0_conv_g_gamma': 7.977,
     'L0_conv_g_beta': 3.724,
     'L0_conv_g_mean': 3.285,
     'L0_conv_g_var': 4.534,
     'L0_conv_g1_gamma': 8.0,
     'L0_conv_g1_beta': 3.519,
     'L0_conv_g1_mean': 2.979,
     'L0_conv_g1_var': 6.611,
     'L2_conv_in_proj_w': 8.0,
     'L2_conv_conv_w': 8.0,
     'L2_conv_x_proj_w': 8.0,
     'L2_conv_dt_proj_w': 8.0,
     'L2_conv_dt_proj_b': 8.0,
     'L2_conv_A_log': 8.0,
     'L2_conv_out_proj_w': 8.0}
    for name, (base, spread) in spreads.items():
        noise = np.random.default_rng([zlib.crc32(name.encode()), seed]).standard_normal(out[name].shape)
        drawn = base * np.exp(spread * noise) if base else spread * noise
        out[name] = jnp.asarray(drawn.astype(out[name].dtype))
    for name, factor in factors.items():
        out[name] = (out[name] * factor).astype(out[name].dtype)
    return out
```

```python
import concourse.bass as bass
from concourse import mybir
from contextlib import ExitStack

fp32 = mybir.dt.float32
bf16 = mybir.dt.bfloat16
ALU = mybir.AluOpType
ACT = mybir.ActivationFunctionType
AX = mybir.AxisListType

B, H, W, C = 8, 32, 32, 64
PAIRS = B // 2
HALVES = PAIRS // 2
L = H * W
P = 128
BLK = L // P
HB = 16
BANK = 512
D_STATE = 16
STEPS = 5
FRAME = (H + 2) * (W + 2)
GN_EPS, BN_EPS, LN_EPS = 1e-5, 1e-3, 1e-5
DT = 0.2

VEC = ["g_gamma", "g_beta", "g_mean", "g_var", "g1_gamma", "g1_beta", "g1_mean", "g1_var",
       "out_gamma", "out_beta", "out_mean", "out_var", "conv_bias", "ln_g", "ln_b", "proj_b",
       "m_conv_b", "m_dt_b", "m_D", "skip"]
V = {n: i for i, n in enumerate(VEC)}
V_WG = len(VEC)
V_CONVW = V_WG + 18
V_ALOG = V_CONVW + 4
NVEC = V_ALOG + D_STATE

MAT = ["ident", "neg_ident", "group_mean", "roll_up", "roll_down", "roll_diff", "dct"]
M = {n: i for i, n in enumerate(MAT)}


def fused_blocks(nc, x, vec, mats, conv_w, in_w, xbc_w, xdt_w, dtp_w, out_w, proj_w, out):
    ctx = ExitStack()
    with ctx:
        def sb(c, name, cols, dt=fp32, parts=P):
            return c.enter_context(nc.sbuf_tensor(name, [parts, cols], dt))

        sems = {}

        def S(name):
            if name not in sems:
                sems[name] = ctx.enter_context(nc.semaphore("s_" + name))
            return sems[name]

        xres = sb(ctx, "xres", PAIRS * L)
        vecs = sb(ctx, "vecs", NVEC + 32)
        mat = sb(ctx, "mat", len(MAT) * P)
        convw = sb(ctx, "convw", 9 * P)
        inw = sb(ctx, "inw", 4 * C)
        xbcw = sb(ctx, "xbcw", 96)
        dtw = sb(ctx, "dtw", P)
        xdtw = sb(ctx, "xdtw", P, parts=4)
        dtpw = sb(ctx, "dtpw", P, parts=4)
        outw = sb(ctx, "outw", C)
        projw = sb(ctx, "projw", P)
        skipI = sb(ctx, "skipI", P)
        diagD = sb(ctx, "diagD", P)
        Amat = sb(ctx, "Amat", D_STATE)
        par = sb(ctx, "par", 16)
        cpow = sb(ctx, "cpow", 16)

        def mt(name):
            return mat[:, M[name] * P:(M[name] + 1) * P]

        def vc(name):
            return vecs[:, V[name]:V[name] + 1]

        ident = mt("ident")
        PS = [ctx.enter_context(nc.psum_tensor(f"ps{i}", [P, 2 * BANK], fp32)) for i in range(4)]

        ctxA = ExitStack()
        diag = sb(ctxA, "diag", 18 * P)
        A = []
        for k in range(2):
            t = {}
            for n, cols in [("fz", FRAME), ("fr", FRAME), ("hw", H * (W + 2)),
                            ("X", (H + 2) * W), ("Y", (H + 2) * W),
                            ("XY", L), ("sden", L), ("R", L), ("Dc", L), ("Kx", L), ("Ky", L), ("g", L), ("g1", L),
                            ("G", L), ("G1", L), ("Pmx", L), ("Pmy", L), ("P0", L), ("Pe", L), ("Sc", L),
                            ("st", 12), ("ag", 8), ("gn", 4)]:
                t[n] = sb(ctxA, f"a{k}_{n}", cols)
            A.append(t)
        ctxA.close()
        sel = ctx.enter_context(nc.sbuf_tensor("sel", [96, 32 * P], bf16))
        c = {}
        for n, cols in [("fz", FRAME), ("X2", L), ("N2", L), ("XC", L), ("SQ", L), ("XN", L), ("XNC", L),
                        ("XI", L), ("XS", L), ("SZ0", L), ("SZ1", L), ("AB", L), ("EX", L), ("UU", L), ("LN", L), ("RX", L),
                        ("DL", L), ("DU", L), ("R1", L), ("YG0", L), ("YG1", L),
                        ("DA0", L), ("DA1", L), ("DB0", L), ("DB1", L), ("HS0", L), ("HS1", L),
                        ("CB0", L), ("CB1", L), ("HC0", L), ("HC1", L),
                        ("X3", L), ("OT", L),
                        ("st", 12), ("ag", 8), ("gn", 4), ("m", 16), ("v", 16), ("r", 16)]:
            c[n] = sb(ctx, "c_" + n, cols)
        BCS = ctx.enter_context(nc.sbuf_tensor("BCS", [96, L], bf16))
        MID = ctx.enter_context(nc.sbuf_tensor("MID", [96, L], bf16))
        V1 = c["XC"]
        N3, T1, A2, T2 = c["N2"], c["XC"], c["SQ"], c["XN"]

        block = ctx.enter_context(nc.Block())

        def img(t):
            return t[:, 0:L].rearrange("p (h w) -> p h w", h=H)

        def frm(t):
            return t[:, 0:FRAME].rearrange("p (h w) -> p h w", h=H + 2)

        def blk(t, k):
            return t[:, k * P:(k + 1) * P]

        def half(t, n):
            return t[:, n * BANK:(n + 1) * BANK]

        def plain(eng):
            eng.sem_inc(S("waited"), 1)

        x_pix = x.rearrange("b (k q) w c -> b (q w) k c", q=4)
        out_v = out.rearrange("b l (kb kq) c -> b kq l kb c", kq=4)

        @block.sync
        def _(sp):
            sp.dma_start(vecs[:, :], vec).then_inc(S("vecs"), 16)
            sp.dma_start(mat[:, :], mats).then_inc(S("mats"), 16)
            for dst, src in [(convw, conv_w), (inw, in_w), (xbcw, xbc_w), (xdtw, xdt_w), (dtpw, dtp_w),
                             (outw, out_w), (projw, proj_w)]:
                sp.dma_start(dst[:, :], src).then_inc(S("weights"), 16)
            with sp.Fori(0, HALVES) as h:
                for k in range(2):
                    sp.wait_ge(S("a_sobel"), 2 * h)
                    for b in range(2):
                        dst = A[k]["fr"][:, 0:L].rearrange("p (k b c) -> p b k c", b=2, c=C)[:, b]
                        sp.dma_start(dst, x_pix[4 * h + 2 * k + b]).then_inc(S(f"a{k}_loaded"), 16)
            with sp.Fori(0, PAIRS) as p:
                sp.wait_ge(S("c_out_tile"), p + 1)
                for b in range(2):
                    for kq in range(4):
                        src = c["OT"][32 * kq:32 * kq + 32, :].rearrange("l (kb b c) -> l b kb c", b=2, c=C)[:, b]
                        sp.dma_start(out_v[2 * p + b][kq], src).then_inc(S("stored"), 16)
            sp.wait_ge(S("stored"), 16 * 8 * PAIRS)

        @block.gpsimd
        def _(pool):
            tt = nc.gpsimd.tensor_tensor
            pool.memset(cpow[:, :], -0.5).then_inc(S("cpow"), 1)
            for k in range(2):
                pool.memset(A[k]["fz"][:, :], 0.0).then_inc(S("a_frame_zero"), 1)
            pool.wait_ge(S("cpow"), 1)
            pool.wait_ge(S("bn_var"), 3)
            tt(par[:, 6:9], par[:, 6:9], cpow[:, 0:3], ALU.pow).then_inc(S("bn_rstd"), 1)
            with pool.Fori(0, HALVES) as h:
                for k in range(2):
                    a = A[k]
                    pool.wait_ge(S("a_gvar"), 2 * h + k + 1)
                    tt(a["gn"][:, 0:1], a["gn"][:, 0:1], cpow[:, 0:1], ALU.pow).then_inc(S("a_grstd"), 1)
                for k in range(2):
                    a = A[k]
                    pool.wait_ge(S("a_XYone"), 2 * h + k + 1)
                    tt(a["XY"][:, 0:L], a["X"][:, 0:L], a["Y"][:, 0:L], ALU.mult).then_inc(S("a_XY"), 1)
                for k in range(2):
                    a = A[k]
                    pool.wait_ge(S("a_D"), 2 * h + k + 1)
                    pool.wait_ge(S(f"a{k}_gg1"), 2 * h + 2)
                    tt(a["G"][:, :], a["g"][:, :], a["Dc"][:, :], ALU.mult).then_inc(S(f"a{k}_G"), 1)
                    tt(a["G1"][:, :], a["g1"][:, :], a["Dc"][:, :], ALU.mult).then_inc(S(f"a{k}_G"), 1)
                for k in range(2):
                    a = A[k]
                    pool.wait_ge(S("a_S"), 2 * h + k + 1)
                    pool.wait_ge(S("a_P0"), 2 * h + k + 1)
                    pool.wait_ge(S("a_Pe"), 2 * h + k + 1)
                    f_in = frm(a["fz"])[:, 1:33, 1:33]
                    tt(img(a["g"]), img(a["P0"]), f_in, ALU.mult).then_inc(S(f"a{k}_Wc"), 1)
                    pool.wait_ge(S(f"a{k}_Wc"), (STEPS + 1) * h + 1)
                    tt(a["G1"][:, :], a["g"][:, :], a["Sc"][:, :], ALU.add).then_inc(S(f"a{k}_U"), 1)
                with pool.Fori(0, STEPS) as t:
                    for k in range(2):
                        a = A[k]
                        pool.wait_ge(S(f"a{k}_h"), (STEPS + 1) * h + t + 1)
                        pool.wait_ge(S(f"a{k}_mix"), STEPS * h + t)
                        pool.wait_ge(S(f"a{k}_U"), (STEPS + 1) * h + t + 1)
                        hc = a["hw"][:, :].rearrange("p (h w) -> p h w", h=H)[:, :, 1:33]
                        tt(img(a["X"]), img(a["Pe"]), hc, ALU.mult).then_inc(S(f"a{k}_e"), 1)
                        tt(img(a["g"]), img(a["P0"]), hc, ALU.mult).then_inc(S(f"a{k}_Wc"), 1)
                    for k in range(2):
                        a = A[k]
                        pool.wait_ge(S(f"a{k}_h"), (STEPS + 1) * h + t + 2)
                        pool.wait_ge(S(f"a{k}_Wc"), (STEPS + 1) * h + t + 2)
                        tt(a["G1"][:, :], a["g"][:, :], a["Sc"][:, :], ALU.add).then_inc(S(f"a{k}_U"), 1)
                for k in range(2):
                    a = A[k]
                    pool.wait_ge(S("a_bnout"), 2 * h + k + 1)
                    xs = xres[:, bass.ds((2 * h + k) * L, L)]
                    tt(xs, xs, a["X"][:, 0:L], ALU.add).then_inc(S("x1"), 1)

            pool.wait_ge(S("x1"), PAIRS)
            pool.memset(c["fz"][:, :], 0.0).then_inc(S("c_frame_zero"), 1)
            with pool.Fori(0, PAIRS) as p:
                for g in range(2):
                    pool.wait_ge(S("c_gvar"), 3 * p + g + 1)
                    tt(c["gn"][:, 0:1], c["gn"][:, 0:1], cpow[:, 0:1], ALU.pow).then_inc(S("c_grstd"), 1)
                pool.wait_ge(S("c_lvar"), 2 * p + 1)
                tt(c["r"][:, :], c["v"][:, :], cpow[:, :], ALU.pow).then_inc(S("c_lrstd"), 1)
                for b in range(2):
                    pool.wait_ge(S("c_sp_parts"), 2 * p + b + 1)
                    tt(c["LN"][:, :], c["LN"][:, :], c["EX"][:, :], ALU.subtract).then_inc(S("c_sp_log"), 1)
                    pool.wait_ge(S("c_sp_log"), 2 * p + b + 1)
                    tt(c["DL"][:, :], c["LN"][:, :], c["RX"][:, :], ALU.add).then_inc(S("c_delta"), 1)
                    pool.wait_ge(S("c_delta"), 2 * p + b + 1)
                    tt(c["DU"][:, :], c["DL"][:, :], c["XS"][:, :], ALU.mult).then_inc(S("c_du"), 1)
                    with pool.Fori(0, D_STATE // 2) as n:
                        for q in range(2):
                            m = (2 * p + b) * D_STATE + 2 * n + q
                            m8 = (2 * p + b) * (D_STATE // 2) + n
                            pool.wait_ge(S(f"c_scan{q}"), m8 + 1)
                            pool.wait_ge(S(f"c_cb{q}"), m8 + 1)
                            pool.wait_ge(S(f"c_sum{q}"), m8)
                            tt(c[f"HC{q}"][:, :], c[f"HS{q}"][:, :], c[f"CB{q}"][:, :], ALU.mult).then_inc(S(f"c_hc{q}"), 1)
                pool.wait_ge(S("c_lvar"), 2 * p + 2)
                tt(c["r"][:, :], c["v"][:, :], cpow[:, :], ALU.pow).then_inc(S("c_lrstd"), 1)
                pool.wait_ge(S("c_gvar"), 3 * p + 3)
                tt(c["gn"][:, 0:1], c["gn"][:, 0:1], cpow[:, 0:1], ALU.pow).then_inc(S("c_grstd"), 1)

        @block.tensor
        def _(pe):
            mm = nc.tensor.matmul
            pe.wait_ge(S("mats"), 16)
            pe.wait_ge(S("weights"), 16 * 7)
            mm(PS[3][:, 0:P], xdtw[:, :], dtpw[:, :], start=True, stop=True).then_inc(S("dtw_ps"), 1)
            pe.wait_ge(S("dtw"), 1)
            pe.wait_ge(S("diag"), 18)
            with pe.Fori(0, HALVES) as h:
                for k in range(2):
                    pe.wait_ge(S(f"a{k}_loaded"), 32 * h + 32)
                    pe.wait_ge(S(f"a{k}_h"), (STEPS + 1) * h)
                    for n in range(BLK):
                        last = nc.tensor.transpose(blk(PS[2 * k], n), blk(A[k]["fr"], n), ident)
                    last.then_inc(S("a_xT"), 1)
                for k in range(2):
                    pe.wait_ge(S("a_stats"), 2 * h + k + 1)
                    pe.wait_ge(S("a_Q5"), 2 * h)
                    mm(PS[2 * k + 1][:, 0:2], mt("group_mean"), A[k]["ag"][:, 0:2], start=True, stop=True).then_inc(S("a_gmean"), 1)
                for k in range(2):
                    fz = frm(A[k]["fz"])
                    pe.wait_ge(S("a_fz"), 2 * h + k + 1)
                    pe.wait_ge(S("a_x"), 2 * h + k + 1)
                    for w in range(2):
                        if w == 1:
                            pe.wait_ge(S("a_gvar"), 2 * h + k + 1)
                        for n in range(2):
                            for tap in range(9):
                                dy, dx = tap // 3, tap % 3
                                last = mm(half(PS[2 * k + w], n), blk(diag, 9 * w + tap),
                                          fz[:, dy + HB * n:dy + HB * n + HB, dx:dx + W],
                                          start=(tap == 0), stop=(tap == 8))
                        last.then_inc(S(f"a_conv{w}"), 1)
                for k in range(2):
                    a = A[k]
                    pe.wait_ge(S(f"a{k}_gg1"), 2 * h + 2)
                    g, ps = img(a["g"]), img(PS[2 * k])
                    for n in range(2):
                        r = slice(HB * n, HB * n + HB)
                        mm(ps[:, r, :], mt("roll_diff"), img(a["g1"])[:, r, :], start=True, stop=False)
                        mm(ps[:, r, 0:31], ident, g[:, r, 1:32], start=False, stop=False)
                        mm(ps[:, r, 31:32], ident, g[:, r, 0:1], start=False, stop=False)
                        mm(ps[:, r, 1:32], mt("neg_ident"), g[:, r, 0:31], start=False, stop=False)
                        last = mm(ps[:, r, 0:1], mt("neg_ident"), g[:, r, 31:32], start=False, stop=True)
                    last.then_inc(S("a_div"), 1)
                for k in range(2):
                    a = A[k]
                    pe.wait_ge(S("a_Pmy"), 2 * h + k + 1)
                    for n in range(2):
                        last = mm(half(PS[2 * k + 1], n), mt("roll_down"), half(a["Pmy"], n), start=True, stop=True)
                    last.then_inc(S("a_rollm"), 1)
                    pe.wait_ge(S("a_Ppy"), 2 * h + k + 1)
                    pe.wait_ge(S("a_Pe"), 2 * h + k + 1)
                    for n in range(2):
                        last = mm(half(PS[2 * k], n), mt("roll_up"), half(a["R"], n), start=True, stop=True)
                    last.then_inc(S("a_rollp"), 1)
                with pe.Fori(0, STEPS) as t:
                    for k in range(2):
                        a = A[k]
                        it = STEPS * h + t
                        for name, mname, src in [("c5", "roll_up", "Pmy"), ("c6", "roll_down", "sden"), ("e", "ident", "X"), ("ab", "ident", "R")]:
                            pe.wait_ge(S(f"a{k}_{name}"), it + 1)
                            if name == "c5":
                                pe.wait_ge(S("a_Q6"), 2 * h + k + 1)
                                pe.wait_ge(S(f"a{k}_h"), (STEPS + 1) * h + t + 1)
                            for n in range(2):
                                last = mm(half(PS[2 * k], n), mt(mname), half(a[src], n), start=(name == "c5"), stop=(name == "ab"))
                        last.then_inc(S(f"a{k}_mix"), 1)

            def transposes(src, dst):
                for n in range(BLK):
                    last = nc.tensor.transpose(blk(dst, n), src(n), ident)
                return last

            def group_mean(stat, g):
                mm(PS[3][:, 0:2], mt("group_mean"), c["ag"][:, 0:2], start=True, stop=True).then_inc(S("c_gmean"), 1)

            with pe.Fori(0, PAIRS) as p:
                pe.wait_ge(S("c_stats"), 3 * p + 1)
                pe.wait_ge(S("c_out_tile"), p)
                group_mean("c_stats0", 0)
                pe.wait_ge(S("c_fz"), p + 1)
                fz = frm(c["fz"])
                for n in range(2):
                    for tap in range(9):
                        dy, dx = tap // 3, tap % 3
                        last = mm(half(PS[0], n), blk(convw, tap), fz[:, dy + HB * n:dy + HB * n + HB, dx:dx + W],
                                  start=(tap == 0), stop=(tap == 8))
                last.then_inc(S("c_conv"), 1)
                pe.wait_ge(S("c_stats"), 3 * p + 2)
                pe.wait_ge(S("c_gvar"), 3 * p + 1)
                group_mean("c_stats1", 1)
                pe.wait_ge(S("c_n2"), p + 1)
                transposes(lambda n: blk(c["N2"], n), PS[1]).then_inc(S("c_n2T"), 1)
                pe.wait_ge(S("c_xn"), p + 1)
                pe.wait_ge(S("c_X2"), p + 1)
                transposes(lambda n: blk(c["XN"], n), PS[0]).then_inc(S("c_xnT"), 1)
                pe.wait_ge(S("c_xnc"), p + 1)
                for b in range(2):
                    i = 2 * p + b
                    rows = slice(C * b, C * b + C)
                    if b == 1:
                        pe.wait_ge(S("c_yg"), i)
                        pe.wait_ge(S("c_cbdone"), i)
                    else:
                        pe.wait_ge(S("c_gvar"), 3 * p + 2)
                    for n in range(2):
                        last = mm(half(PS[2], n), inw[rows, 0:P], half(c["XNC"], n)[rows, :], start=True, stop=True)
                    last.then_inc(S("c_xi"), 1)
                    for n in range(2):
                        last = mm(half(PS[3], n), inw[rows, P:2 * P], half(c["XNC"], n)[rows, :], start=True, stop=True)
                    last.then_inc(S("c_z"), 1)
                    pe.wait_ge(S("c_xs"), i + 1)
                    for n in range(2):
                        last = mm(half(PS[2], n), dtw[:, :], half(c["XS"], n), start=True, stop=True)
                    last.then_inc(S("c_dt"), 1)
                    pe.wait_ge(S("c_sz"), i + 1)
                    for n in range(2):
                        last = mm(half(PS[3], n)[0:96, :], xbcw[:, :], half(c["XS"], n), start=True, stop=True)
                    last.then_inc(S("c_bc"), 1)
                    pe.wait_ge(S("c_bc_hi"), 2 * i + 2)
                    pe.wait_ge(S("c_dtread"), 2 * i + 2)
                    pe.wait_ge(S("c_bcs"), i + 1)
                    for n in range(2):
                        mm(half(PS[3], n), diagD[:, :], half(c["XS"], n), start=True, stop=False, skip_group_check=True)
                    with pe.Fori(0, D_STATE // 2) as n2:
                        for q in range(2):
                            m8 = (D_STATE // 2) * i + n2
                            pe.wait_ge(S(f"c_dbu{q}"), m8)
                            selB = sel[:, bass.ds((2 * n2 + q) * P, P)]
                            selC = sel[:, bass.ds((2 * n2 + q + D_STATE) * P, P)]
                            for n in range(2):
                                last = mm(half(PS[q], n), selB, half(BCS, n), start=True, stop=True)
                            last.then_inc(S(f"c_bb{q}"), 1)
                            if q == 0:
                                pe.wait_ge(S("c_cb1"), m8)
                            else:
                                pe.wait_ge(S("c_cb0"), m8 + 1)
                            for n in range(2):
                                last = mm(half(PS[2], n), selC, half(BCS, n), start=True, stop=True)
                            last.then_inc(S(f"c_cps{q}"), 1)
                            pe.wait_ge(S(f"c_hc{q}"), m8 + 1)
                            for n in range(2):
                                last = mm(half(PS[3], n), ident, half(c[f"HC{q}"], n), start=False, stop=True, skip_group_check=True)
                            last.then_inc(S(f"c_sum{q}"), 1)
                pe.wait_ge(S("c_yg"), 2 * p + 2)
                for n in range(BLK):
                    mm(blk(PS[0], n), blk(c["XNC"], n), skipI[:, :], start=(n % 4 == 0), stop=False, skip_group_check=True)
                for n in range(BLK):
                    for b in range(2):
                        last = mm(blk(PS[0], n)[:, C * b:C * b + C], blk(c[f"YG{b}"], n), outw[:, :],
                                  start=False, stop=True, skip_group_check=True)
                last.then_inc(S("c_mo"), 1)
                pe.wait_ge(S("c_xn2"), p + 1)
                transposes(lambda n: blk(c["XN"], n), PS[1]).then_inc(S("c_xn2T"), 1)
                pe.wait_ge(S("c_v1"), p + 1)
                for n in range(2):
                    last = mm(half(PS[0], n), projw[:, :], half(V1, n), start=True, stop=True)
                last.then_inc(S("c_proj"), 1)
                pe.wait_ge(S("c_stats"), 3 * p + 3)
                group_mean("c_stats2", 2)
                pe.wait_ge(S("c_n3"), p + 1)
                transposes(lambda n: blk(N3, n), PS[1]).then_inc(S("c_n3T"), 1)
                pe.wait_ge(S("c_t1"), p + 1)
                for n in range(BLK):
                    last = mm(blk(PS[0], n), blk(T1, n), mt("dct"), start=True, stop=True, skip_group_check=True)
                last.then_inc(S("c_dct1"), 1)
                pe.wait_ge(S("c_a2"), p + 1)
                transposes(lambda n: blk(A2, n), PS[1]).then_inc(S("c_a2T"), 1)
                pe.wait_ge(S("c_t2"), p + 1)
                pe.wait_ge(S("c_gvar"), 3 * p + 3)
                for n in range(BLK):
                    if n % 4 == 0:
                        mm(half(PS[3], n // 4), mt("dct"), half(T2, n // 4), start=True, stop=False, skip_group_check=True)
                    last = mm(blk(PS[3], n), blk(c["X3"], n), ident, start=False, stop=True, skip_group_check=True)
                last.then_inc(S("c_final"), 1)

        @block.scalar
        def _(act):
            def av(out_, in_, func, scale=1.0, bias=0.0):
                return nc.scalar.activation(out_, in_, func, bias=bias, scale=scale)

            act.wait_ge(S("dtw_ps"), 1)
            av(dtw[:, :], PS[3][:, 0:P], ACT.Identity).then_inc(S("dtw"), 1)
            act.wait_ge(S("vecs"), 16)
            av(Amat[:, :], vecs[:, V_ALOG:V_ALOG + D_STATE], ACT.Exp).then_inc(S("Aexp"), 1)
            act.wait_ge(S("par"), 6)
            with act.Fori(0, HALVES) as h:
                for k in range(2):
                    act.wait_ge(S("a_xT"), 2 * h + k + 1)
                    plain(act)
                    av(xres[:, bass.ds((2 * h + k) * L, L)], PS[2 * k][:, :], ACT.Identity).then_inc(S("a_x"), 1)
                for k in range(2):
                    a = A[k]
                    act.wait_ge(S("a_gshift"), 2 * h + k + 1)
                    act.wait_ge(S("a_frame_zero"), 2)
                    act.wait_ge(S("a_x"), 2 * h + k + 1)
                    plain(act)
                    xs = xres[:, bass.ds((2 * h + k) * L, L)].rearrange("p (h w) -> p h w", h=H)
                    av(frm(a["fz"])[:, 1:33, 1:33], xs, ACT.Identity, a["gn"][:, 0:1], a["gn"][:, 1:2]).then_inc(S("a_fz"), 1)
                    fr = frm(a["fr"])
                    av(fr[:, 1:33, 1:33], xs, ACT.Identity, a["gn"][:, 0:1], a["gn"][:, 1:2]).then_inc(S(f"a{k}_fri"), 1)
                    hw = a["hw"][:, :].rearrange("p (h w) -> p h w", h=H)
                    av(hw[:, :, 1:33], xs, ACT.Identity, a["gn"][:, 0:1], a["gn"][:, 1:2]).then_inc(S(f"a{k}_h"), 1)
                    act.wait_ge(S(f"a{k}_fri"), 4 * h + 1)
                    av(fr[:, 1:33, 0:1], fr[:, 1:33, 2:3], ACT.Identity).then_inc(S(f"a{k}_fri"), 1)
                    av(fr[:, 1:33, 33:34], fr[:, 1:33, 31:32], ACT.Identity).then_inc(S(f"a{k}_fri"), 1)
                    act.wait_ge(S(f"a{k}_fri"), 4 * h + 3)
                    av(fr[:, 0:1, :], fr[:, 2:3, :], ACT.Identity)
                    av(fr[:, 33:34, :], fr[:, 31:32, :], ACT.Identity).then_inc(S(f"a{k}_fri"), 1)
                for k in range(2):
                    a = A[k]
                    act.wait_ge(S("a_conv0"), 2 * h + k + 1)
                    av(a["g"][:, :], PS[2 * k][:, :], ACT.Relu, par[:, 0:1], par[:, 1:2]).then_inc(S(f"a{k}_gg1"), 1)
                    act.wait_ge(S("a_conv1"), 2 * h + k + 1)
                    av(a["g1"][:, :], PS[2 * k + 1][:, :], ACT.Relu, par[:, 2:3], par[:, 3:4]).then_inc(S(f"a{k}_gg1"), 1)
                for k in range(2):
                    a = A[k]
                    act.wait_ge(S("a_sobel"), 2 * h + k + 1)
                    av(a["Dc"][:, 0:L], a["R"][:, 0:L], ACT.Square, 0.5).then_inc(S(f"a{k}_sq"), 1)
                    av(a["Kx"][:, 0:L], a["XY"][:, 0:L], ACT.Square, 0.5).then_inc(S(f"a{k}_sq"), 1)
                    act.wait_ge(S(f"a{k}_sq"), 2 * h + 2)
                    av(a["X"][:, 0:L], a["Dc"][:, 0:L], ACT.Identity, 1.0, 1.0)
                    av(a["Y"][:, 0:L], a["Kx"][:, 0:L], ACT.Identity, 1.0, 1.0).then_inc(S("a_XYone"), 1)
                for k in range(2):
                    a = A[k]
                    act.wait_ge(S("a_rollm"), 2 * h + k + 1)
                    act.wait_ge(S("a_Pm"), 2 * h + k + 1)
                    av(a["Kx"][:, :], PS[2 * k + 1][:, :], ACT.Identity).then_inc(S("a_Q5"), 1)
                    act.wait_ge(S("a_rollp"), 2 * h + k + 1)
                    av(a["Ky"][:, :], PS[2 * k][:, :], ACT.Identity).then_inc(S("a_Q6"), 1)
                with act.Fori(0, STEPS) as t:
                    for k in range(2):
                        hw = A[k]["hw"][:, :].rearrange("p (h w) -> p h w", h=H)
                        act.wait_ge(S(f"a{k}_h"), (STEPS + 1) * h + t + 1)
                        av(hw[:, :, 0:1], hw[:, :, 32:33], ACT.Identity)
                        av(hw[:, :, 33:34], hw[:, :, 1:2], ACT.Identity).then_inc(S(f"a{k}_wrap"), 1)
                for k in range(2):
                    a = A[k]
                    hw = a["hw"][:, :].rearrange("p (h w) -> p h w", h=H)
                    act.wait_ge(S(f"a{k}_h"), (STEPS + 1) * h + STEPS + 1)
                    av(img(a["X"]), hw[:, :, 1:33], ACT.Relu, par[:, 4:5], par[:, 5:6]).then_inc(S("a_bnout"), 1)

            act.wait_ge(S("x1"), PAIRS)
            with act.Fori(0, PAIRS) as p:
                def gnorm(out_, in_, g):
                    act.wait_ge(S("c_gshift"), 3 * p + g + 1)
                    plain(act)
                    return av(out_, in_, ACT.Identity, c["gn"][:, 0:1], c["gn"][:, 1:2])

                act.wait_ge(S("c_frame_zero"), 1)
                xs = xres[:, bass.ds(p * L, L)].rearrange("p (h w) -> p h w", h=H)
                gnorm(frm(c["fz"])[:, 1:33, 1:33], xs, 0).then_inc(S("c_fz"), 1)
                gnorm(c["N2"][:, :], c["X2"][:, :], 1).then_inc(S("c_n2"), 1)
                act.wait_ge(S("c_xc"), 2 * p + 1)
                av(c["SQ"][:, :], c["XC"][:, :], ACT.Square).then_inc(S("c_csq"), 1)
                act.wait_ge(S("c_xnT"), p + 1)
                av(c["XNC"][:, :], PS[0][:, :], ACT.Identity, vc("ln_g"), vc("ln_b")).then_inc(S("c_xnc"), 1)
                for b in range(2):
                    i = 2 * p + b
                    act.wait_ge(S("c_z"), i + 1)
                    av(c[f"SZ{b}"][:, :], PS[3][:, :], ACT.Silu).then_inc(S("c_sz"), 1)
                    act.wait_ge(S("c_cconv"), i + 1)
                    av(c["XS"][:, :], c["XI"][:, :], ACT.Silu, 1.0, vc("m_conv_b")).then_inc(S("c_xs"), 1)
                    act.wait_ge(S("c_dt"), i + 1)
                    av(c["AB"][:, :], PS[2][:, :], ACT.Abs, 1.0, vc("m_dt_b")).then_inc(S("c_dtread"), 1)
                    act.wait_ge(S("c_dtread"), 2 * i + 1)
                    av(c["EX"][:, :], c["AB"][:, :], ACT.Exp, -1.0).then_inc(S("c_ex"), 1)
                    act.wait_ge(S("c_ex"), i + 1)
                    av(c["UU"][:, :], c["EX"][:, :], ACT.Identity, 1.0, 1.0).then_inc(S("c_uu"), 1)
                    act.wait_ge(S("c_uu"), i + 1)
                    av(c["LN"][:, :], c["UU"][:, :], ACT.Ln).then_inc(S("c_ln"), 1)
                    act.wait_ge(S("c_bc"), i + 1)
                    act.wait_ge(S("c_sel_free"), i)
                    av(BCS[:, :], PS[3][0:96, :], ACT.Identity).then_inc(S("c_bc_hi"), 1)
                    act.wait_ge(S("c_bc_hi"), 2 * i + 2)
                    av(MID[:, :], c["R1"][0:96, :], ACT.Identity).then_inc(S("c_bc_mid"), 1)
                    av(BCS[32:64, :], c["R1"][32:64, :], ACT.Identity).then_inc(S("c_bc_mid"), 1)
                    act.wait_ge(S("c_delta"), i + 1)
                    plain(act)
                    with act.Fori(0, D_STATE // 2) as n2:
                        for q in range(2):
                            m8 = (D_STATE // 2) * i + n2
                            act.wait_ge(S(f"c_scan{q}"), m8)
                            plain(act)
                            av(c[f"DA{q}"][:, :], c["DL"][:, :], ACT.Exp, Amat[:, bass.ds(2 * n2 + q, 1)]).then_inc(S(f"c_da{q}"), 1)
                            act.wait_ge(S(f"c_cps{q}"), m8 + 1)
                            act.wait_ge(S(f"c_hc{q}"), m8)
                            av(c[f"CB{q}"][:, :], PS[2][:, :], ACT.Identity).then_inc(S(f"c_cb{q}"), 1)
                    act.wait_ge(S("c_cb1"), (D_STATE // 2) * (i + 1))
                    act.sem_inc(S("c_cbdone"), 1)
                act.wait_ge(S("c_xc"), 2 * p + 2)
                av(c["SQ"][:, :], c["XC"][:, :], ACT.Square).then_inc(S("c_csq"), 1)
                act.wait_ge(S("c_xn2T"), p + 1)
                av(V1[:, :], PS[1][:, :], ACT.Identity, vc("ln_g"), vc("ln_b")).then_inc(S("c_v1"), 1)
                gnorm(N3[:, :], c["X3"][:, :], 2).then_inc(S("c_n3"), 1)
                act.wait_ge(S("c_n3T"), p + 1)
                av(T1[:, :], PS[1][:, :], ACT.Identity).then_inc(S("c_t1"), 1)
                act.wait_ge(S("c_dct1"), p + 1)
                av(A2[:, :].rearrange("p (k w) -> p w k", k=H), PS[0][:, :].rearrange("p (w k) -> p w k", w=W), ACT.Identity).then_inc(S("c_a2"), 1)
                act.wait_ge(S("c_a2T"), p + 1)
                av(T2[:, :], PS[1][:, :], ACT.Identity).then_inc(S("c_t2"), 1)
                act.wait_ge(S("c_final"), p + 1)
                act.wait_ge(S("stored"), 16 * 8 * p)
                av(c["OT"][:, :], PS[3][:, :], ACT.Identity).then_inc(S("c_out_tile"), 1)

        @block.vector
        def _(dve):
            tt = nc.vector.tensor_tensor
            stt = nc.vector.scalar_tensor_tensor
            ts = nc.vector.tensor_scalar
            chain = [0]

            def link(ins):
                chain[0] += 1
                ins.then_inc(S("setup_step"), 1)
                dve.wait_ge(S("setup_step"), chain[0])

            dve.wait_ge(S("vecs"), 16)
            for n, name in enumerate(["g", "g1", "out"]):
                ts(par[:, 6 + n:7 + n], vc(name + "_var"), BN_EPS, None, ALU.add).then_inc(S("bn_var"), 1)
            dve.wait_ge(S("mats"), 16)
            for t in range(18):
                ts(blk(diag, t), ident, vecs[:, V_WG + t:V_WG + t + 1], None, ALU.mult).then_inc(S("diag"), 1)
            ts(skipI[:, :], ident, vc("skip"), None, ALU.mult)
            ts(diagD[:, :], ident, vc("m_D"), None, ALU.mult).then_inc(S("diag"), 1)
            dve.wait_ge(S("Aexp"), 1)
            link(ts(Amat[:, :], Amat[:, :], -1.0, None, ALU.mult))
            dve.wait_ge(S("bn_rstd"), 1)
            for n, (name, f) in enumerate([("g", DT), ("g1", DT), ("out", 1.0)]):
                link(stt(par[:, 9:10], vc(name + "_gamma"), f, par[:, 6 + n:7 + n], ALU.mult, ALU.mult))
                link(tt(par[:, 10:11], vc(name + "_mean"), par[:, 9:10], ALU.mult))
                ts(par[:, 2 * n:2 * n + 1], par[:, 9:10], 1.0, None, ALU.mult).then_inc(S("par"), 1)
                stt(par[:, 2 * n + 1:2 * n + 2], vc(name + "_beta"), f, par[:, 10:11], ALU.mult, ALU.subtract).then_inc(S("par"), 1)
                dve.wait_ge(S("par"), 2 * n + 2)

            def stats(src, t, step, n0, done):
                nc.vector.bn_stats(t["st"][:, 0:6], src[0]).then_inc(step, 1)
                nc.vector.bn_stats(t["st"][:, 6:12], src[1]).then_inc(step, 1)
                dve.wait_ge(step, n0 + 2)
                plain(dve)
                nc.vector.bn_aggr(t["ag"][:, 0:2], t["st"][:, :]).then_inc(step, 1)
                dve.wait_ge(step, n0 + 3)
                stt(t["ag"][:, 1:2], t["ag"][:, 0:1], t["ag"][:, 0:1], t["ag"][:, 1:2], ALU.mult, ALU.add).then_inc(done, 1)

            def group_var(ps, t, step, n0, gvar, grstd, n1, shift):
                ts(t["ag"][:, 2:4], ps[:, 0:2], 1.0, None, ALU.mult).then_inc(step, 1)
                dve.wait_ge(step, n0 + 1)
                stt(t["ag"][:, 4:5], t["ag"][:, 2:3], t["ag"][:, 2:3], t["ag"][:, 3:4], ALU.mult, ALU.subtract).then_inc(step, 1)
                dve.wait_ge(step, n0 + 2)
                ts(t["gn"][:, 0:1], t["ag"][:, 4:5], -1.0, GN_EPS, ALU.mult, ALU.add).then_inc(gvar, 1)
                dve.wait_ge(grstd, n1)
                stt(t["gn"][:, 1:2], t["ag"][:, 2:3], -1.0, t["gn"][:, 0:1], ALU.mult, ALU.mult).then_inc(shift, 1)

            with dve.Fori(0, HALVES) as h:
                for k in range(2):
                    a = A[k]
                    dve.wait_ge(S("a_x"), 2 * h + k + 1)
                    xs = [xres[:, bass.ds((2 * h + k) * L + BANK * n, BANK)] for n in range(2)]
                    stats(xs, a, S(f"a{k}_step"), 5 * h, S("a_stats"))
                for k in range(2):
                    a = A[k]
                    dve.wait_ge(S("a_gmean"), 2 * h + k + 1)
                    group_var(PS[2 * k + 1], a, S(f"a{k}_step"), 5 * h + 3, S("a_gvar"), S("a_grstd"), 2 * h + k + 1, S("a_gshift"))
                for k in range(2):
                    a = A[k]
                    fr = frm(a["fr"])
                    X = a["X"][:, :].rearrange("p (h w) -> p h w", w=W)
                    Y = a["Y"][:, :].rearrange("p (h w) -> p h w", w=W)
                    dve.wait_ge(S(f"a{k}_fri"), 4 * h + 4)
                    tt(X, fr[:, :, 0:32], fr[:, :, 2:34], ALU.add).then_inc(S(f"a{k}_sob"), 1)
                    dve.wait_ge(S(f"a{k}_sob"), 4 * h + 1)
                    stt(X, fr[:, :, 1:33], 2.0, X, ALU.mult, ALU.add).then_inc(S(f"a{k}_sob"), 1)
                    tt(Y, fr[:, :, 2:34], fr[:, :, 0:32], ALU.subtract).then_inc(S(f"a{k}_sob"), 1)
                    dve.wait_ge(S(f"a{k}_sob"), 4 * h + 3)
                    tt(img(a["R"]), X[:, 2:34, :], X[:, 0:32, :], ALU.subtract)
                    tt(img(a["XY"]), Y[:, 0:32, :], Y[:, 2:34, :], ALU.add).then_inc(S(f"a{k}_sob"), 1)
                    dve.wait_ge(S(f"a{k}_sob"), 4 * h + 4)
                    stt(img(a["XY"]), Y[:, 1:33, :], 2.0, img(a["XY"]), ALU.mult, ALU.add).then_inc(S("a_sobel"), 1)
                for k in range(2):
                    a = A[k]
                    n0 = 5 * h

                    def st(ins, sem=None):
                        return ins.then_inc(S(f"a{k}_coef"), 1)
                    dve.wait_ge(S("a_XYone"), 2 * h + k + 1)
                    st(tt(a["sden"][:, :], a["X"][:, 0:L], a["Y"][:, 0:L], ALU.add))
                    dve.wait_ge(S("a_XY"), 2 * h + k + 1)
                    dve.wait_ge(S(f"a{k}_coef"), n0 + 1)
                    st(stt(a["sden"][:, :], a["sden"][:, :], 2 * DT, a["XY"][:, 0:L], ALU.mult, ALU.add))
                    dve.wait_ge(S(f"a{k}_coef"), n0 + 2)
                    st(nc.vector.reciprocal(a["R"][:, :], a["sden"][:, :]))
                    dve.wait_ge(S(f"a{k}_coef"), n0 + 3)
                    tt(a["Dc"][:, :], a["XY"][:, 0:L], a["R"][:, :], ALU.mult).then_inc(S("a_D"), 1)
                    stt(a["Kx"][:, :], a["Y"][:, 0:L], 2 * DT, a["R"][:, :], ALU.mult, ALU.mult)
                    st(stt(a["Ky"][:, :], a["X"][:, 0:L], 2 * DT, a["R"][:, :], ALU.mult, ALU.mult))
                    dve.wait_ge(S(f"a{k}_coef"), n0 + 4)
                    st(tt(a["P0"][:, :], a["Kx"][:, :], a["Ky"][:, :], ALU.add))
                    dve.wait_ge(S("a_D"), 2 * h + k + 1)
                    dve.wait_ge(S(f"a{k}_coef"), n0 + 5)
                    tt(a["P0"][:, :], a["Dc"][:, :], a["P0"][:, :], ALU.subtract).then_inc(S("a_P0"), 1)
                    dve.wait_ge(S(f"a{k}_G"), 2 * h + 2)
                    tt(a["Pmy"][:, :], a["Ky"][:, :], a["G1"][:, :], ALU.subtract).then_inc(S("a_Pmy"), 1)
                    tt(a["R"][:, :], a["Ky"][:, :], a["G1"][:, :], ALU.add).then_inc(S("a_Ppy"), 1)
                    tt(a["Pmx"][:, :], a["Kx"][:, :], a["G"][:, :], ALU.subtract)
                    tt(a["G"][:, :], a["Kx"][:, :], a["G"][:, :], ALU.add).then_inc(S("a_Pm"), 1)
                    dve.wait_ge(S("a_div"), 2 * h + k + 1)
                    tt(a["Pe"][:, :], a["Dc"][:, :], PS[2 * k][:, :], ALU.mult).then_inc(S("a_Pe"), 1)
                    stt(img(a["Sc"]), frm(a["fz"])[:, 1:33, 1:33], 2 * DT, img(a["Dc"]), ALU.mult, ALU.mult).then_inc(S("a_S"), 1)
                with dve.Fori(0, STEPS) as t:
                    it = STEPS * h + t
                    for k in range(2):
                        a = A[k]
                        hw = a["hw"][:, :].rearrange("p (h w) -> p h w", h=H)
                        hc = hw[:, :, 1:33]
                        dve.wait_ge(S("a_Q6"), 2 * h + k + 1)
                        dve.wait_ge(S(f"a{k}_mix"), it)
                        dve.wait_ge(S(f"a{k}_h"), (STEPS + 1) * h + t + 1)
                        tt(img(a["Pmy"]), img(a["Kx"]), hc, ALU.mult).then_inc(S(f"a{k}_c5"), 1)
                        tt(img(a["sden"]), img(a["Ky"]), hc, ALU.mult).then_inc(S(f"a{k}_c6"), 1)
                        dve.wait_ge(S(f"a{k}_wrap"), it + 1)
                        tt(img(a["R"]), img(a["Pmx"]), hw[:, :, 0:32], ALU.mult)
                        tt(img(a["XY"]), img(a["G"]), hw[:, :, 2:34], ALU.mult).then_inc(S(f"a{k}_abm"), 1)
                        dve.wait_ge(S(f"a{k}_abm"), it + 1)
                        tt(a["R"][:, :], a["R"][:, :], a["XY"][:, :], ALU.add).then_inc(S(f"a{k}_ab"), 1)
                    for k in range(2):
                        a = A[k]
                        hc = a["hw"][:, :].rearrange("p (h w) -> p h w", h=H)[:, :, 1:33]
                        dve.wait_ge(S(f"a{k}_mix"), it + 1)
                        dve.wait_ge(S(f"a{k}_U"), (STEPS + 1) * h + t + 1)
                        dve.wait_ge(S(f"a{k}_Wc"), (STEPS + 1) * h + t + 2)
                        tt(hc, img(PS[2 * k]), img(a["G1"]), ALU.add).then_inc(S(f"a{k}_h"), 1)

            dve.wait_ge(S("x1"), PAIRS)
            nc.vector.tensor_copy(sel[:, :].rearrange("k (j m) -> k j m", m=P),
                                  vecs[0:96, NVEC:NVEC + 32].unsqueeze(2).to_broadcast([96, 32, P])).then_inc(S("sel"), 1)

            with dve.Fori(0, PAIRS) as p:
                xs = [xres[:, bass.ds(p * L + BANK * n, BANK)] for n in range(2)]

                def gn(src, g):
                    stats(src, c, S("c_step"), 15 * p + 5 * g, S("c_stats"))
                    dve.wait_ge(S("c_gmean"), 3 * p + g + 1)
                    group_var(PS[3], c, S("c_step"), 15 * p + 5 * g + 3, S("c_gvar"), S("c_grstd"), 3 * p + g + 1, S("c_gshift"))

                gn(xs, 0)
                dve.wait_ge(S("c_conv"), p + 1)
                stt(c["X2"][:, :], PS[0][:, :], vc("conv_bias"), xres[:, bass.ds(p * L, L)], ALU.add, ALU.add).then_inc(S("c_X2"), 1)
                dve.wait_ge(S("c_X2"), p + 1)
                gn([half(c["X2"], n) for n in range(2)], 1)

                def layer_norm(ps, g):
                    n0 = 6 * p + 3 * g
                    step = S("c_lstep")
                    pv = ps[:, :].rearrange("p (g c) -> p g c", c=C)
                    xc = c["XC"][:, :].rearrange("p (g c) -> p g c", c=C)
                    nc.vector.reduce_sum(c["m"][:, :], pv, axis=AX.X).then_inc(step, 1)
                    dve.wait_ge(step, n0 + 1)
                    ts(c["m"][:, :], c["m"][:, :], 1.0 / C, None, ALU.mult).then_inc(step, 1)
                    dve.wait_ge(step, n0 + 2)
                    tt(xc, pv, c["m"][:, :].unsqueeze(2).to_broadcast([P, 16, C]), ALU.subtract).then_inc(S("c_xc"), 1)
                    dve.wait_ge(S("c_csq"), 2 * p + g + 1)
                    nc.vector.reduce_sum(c["v"][:, :], c["SQ"][:, :].rearrange("p (g c) -> p g c", c=C), axis=AX.X).then_inc(step, 1)
                    dve.wait_ge(step, n0 + 3)
                    ts(c["v"][:, :], c["v"][:, :], 1.0 / C, LN_EPS, ALU.mult, ALU.add).then_inc(S("c_lvar"), 1)
                    dve.wait_ge(S("c_lrstd"), 2 * p + g + 1)
                    return tt(c["XN"][:, :].rearrange("p (g c) -> p g c", c=C), xc,
                              c["r"][:, :].unsqueeze(2).to_broadcast([P, 16, C]), ALU.mult)

                dve.wait_ge(S("c_n2T"), p + 1)
                layer_norm(PS[1], 0).then_inc(S("c_xn"), 1)
                for b in range(2):
                    i = 2 * p + b
                    dve.wait_ge(S("c_xi"), i + 1)
                    w = [vecs[:, V_CONVW + t:V_CONVW + t + 1] for t in range(4)]
                    ts(c["XI"][:, :], PS[2][:, :], w[3], None, ALU.mult).then_inc(S("c_cstep"), 1)
                    for t in range(1, 4):
                        dve.wait_ge(S("c_cstep"), 3 * i + t)
                        stt(c["XI"][:, t:L], PS[2][:, 0:L - t], w[3 - t], c["XI"][:, t:L], ALU.mult, ALU.add)\
                            .then_inc(S("c_cstep") if t < 3 else S("c_cconv"), 1)
                    dve.wait_ge(S("c_dtread"), 2 * i + 1)
                    ts(c["RX"][:, :], PS[2][:, :], vc("m_dt_b"), 0.0, ALU.add, ALU.max).then_inc(S("c_dtread"), 1)
                    dve.wait_ge(S("c_ln"), i + 1)
                    stt(c["EX"][:, :], c["UU"][:, :], -1.0, c["EX"][:, :], ALU.add, ALU.subtract).then_inc(S("c_sp_parts"), 1)
                    dve.wait_ge(S("c_bc_hi"), 2 * i + 1)
                    tt(c["R1"][0:96, :], PS[3][0:96, :], BCS[:, :], ALU.subtract).then_inc(S("c_bc_hi"), 1)
                    dve.wait_ge(S("c_bc_mid"), 2 * i + 2)
                    dve.wait_ge(S("c_bc_hi"), 2 * i + 2)
                    tt(BCS[64:96, :], c["R1"][64:96, :], MID[64:96, :], ALU.subtract).then_inc(S("c_bcs"), 1)
                    dve.wait_ge(S("c_du"), i + 1)
                    plain(dve)
                    with dve.Fori(0, D_STATE // 2) as n2:
                        for q in range(2):
                            m8 = (D_STATE // 2) * i + n2
                            dve.wait_ge(S(f"c_bb{q}"), m8 + 1)
                            dve.wait_ge(S(f"c_scan{q}"), m8)
                            tt(c[f"DB{q}"][:, :], c["DU"][:, :], PS[q][:, :], ALU.mult).then_inc(S(f"c_dbu{q}"), 1)
                            dve.wait_ge(S(f"c_da{q}"), m8 + 1)
                            dve.wait_ge(S(f"c_dbu{q}"), m8 + 1)
                            dve.wait_ge(S(f"c_hc{q}"), m8)
                            nc.vector.tensor_tensor_scan(c[f"HS{q}"][:, :], c[f"DA{q}"][:, :], c[f"DB{q}"][:, :], 0.0,
                                                         ALU.mult, ALU.add).then_inc(S(f"c_scan{q}"), 1)
                    dve.wait_ge(S("c_sum1"), (D_STATE // 2) * (i + 1))
                    tt(c[f"YG{b}"][:, :], PS[3][:, :], c[f"SZ{b}"][:, :], ALU.mult).then_inc(S("c_yg"), 1)
                    dve.sem_inc(S("c_sel_free"), 1)
                dve.wait_ge(S("c_mo"), p + 1)
                layer_norm(PS[0], 1).then_inc(S("c_xn2"), 1)
                dve.wait_ge(S("c_proj"), p + 1)
                stt(c["X3"][:, :].rearrange("p (w h) -> p h w", w=W), img(PS[0]), vc("proj_b"), img(c["X2"]), ALU.add, ALU.add).then_inc(S("c_X3"), 1)
                dve.wait_ge(S("c_X3"), p + 1)
                gn([half(c["X3"], n) for n in range(2)], 2)


def kernel(**inputs):
    import numpy as np
    import concourse.bacc as bacc
    from concourse.bass_utils import run_bass_kernel_spmd

    v = {k: np.asarray(a) for k, a in inputs.items()}

    def two(a):
        return np.concatenate([a, a], axis=0)

    cols = []
    for n in VEC:
        if n[0] in "go" and n != "skip":
            cols.append(two(v["L0_conv_" + n]))
        elif n == "conv_bias":
            cols.append(two(v["L1_conv_bias"]))
        elif n in ("ln_g", "ln_b", "proj_b"):
            cols.append(two(v["L2_conv_" + n]))
        elif n == "m_conv_b":
            cols.append(v["L2_conv_conv_b"])
        elif n == "m_dt_b":
            cols.append(v["L2_conv_dt_proj_b"])
        elif n == "m_D":
            cols.append(v["L2_conv_D"])
        else:
            cols.append(np.broadcast_to(v["L2_conv_skip_scale"], (P,)))
    wg = v["L0_conv_wg"].reshape(9, C).T
    wg1 = v["L0_conv_wg1"].reshape(9, C).T
    row32 = np.zeros((P, 32), np.float32)
    row32[np.arange(P), np.arange(P) % 32] = 1.0
    vec = np.concatenate([np.stack(cols, axis=1), two(wg), two(wg1), v["L2_conv_conv_w"], v["L2_conv_A_log"], row32], axis=1)

    r = np.arange(P)
    eye = np.eye(P, dtype=np.float32)
    group = (r[:, None] // 2 == r[None, :] // 2).astype(np.float32) * np.float32(0.5)
    prev = (r // C) * C + (r % C - 1) % C
    nxt = (r // C) * C + (r % C + 1) % C
    up = np.zeros((P, P), np.float32)
    up[prev, r] = 1.0
    down = np.zeros((P, P), np.float32)
    down[nxt, r] = 1.0
    n = np.arange(H)
    m = np.cos(np.pi * (n[None, :] + 0.5) * n[:, None] / H) * np.sqrt(2.0 / H)
    m[0] *= 1.0 / np.sqrt(2.0)
    dct = np.zeros((P, P), np.float32)
    for q in range(4):
        dct[q * H:(q + 1) * H, q * H:(q + 1) * H] = m.T
    mats = np.concatenate([eye, -eye, group, up, down, down - up, dct], axis=1).astype(np.float32)

    conv = v["L1_conv_kernel"].reshape(9, C, C)
    conv_w = np.zeros((P, 9, P), np.float32)
    proj_w = np.zeros((P, P), np.float32)
    for b in range(2):
        s = slice(b * C, b * C + C)
        conv_w[s, :, s] = conv.transpose(1, 0, 2)
        proj_w[s, s] = v["L2_conv_proj_w"].T
    in_w = two(v["L2_conv_in_proj_w"].T)
    xw = v["L2_conv_x_proj_w"]
    xbc_w = np.concatenate([xw[4:].T] * 3, axis=1)

    arrays = {"x": v["x"], "vec": vec, "mats": mats, "conv_w": conv_w.reshape(P, 9 * P), "in_w": in_w,
              "xbc_w": xbc_w, "xdt_w": xw[:4], "dtp_w": v["L2_conv_dt_proj_w"].T,
              "out_w": v["L2_conv_out_proj_w"].T, "proj_w": proj_w}
    arrays = {k: np.ascontiguousarray(a) for k, a in arrays.items()}

    nc = bacc.Bacc("TRN2", target_bir_lowering=False, num_devices=1)
    args = [nc.dram_tensor(k, a.shape, mybir.dt.from_np(a.dtype), kind="ExternalInput").ap() for k, a in arrays.items()]
    out = nc.dram_tensor("out", (B, H, W, C), fp32, kind="ExternalOutput").ap()
    fused_blocks(nc, *args, out)
    res = run_bass_kernel_spmd(nc, [arrays], core_ids=[0])
    return res.results[0]["out"]
```

```python
import concourse.bass as bass
from concourse import mybir
from contextlib import ExitStack

fp32 = mybir.dt.float32
bf16 = mybir.dt.bfloat16
ALU = mybir.AluOpType
ACT = mybir.ActivationFunctionType
AX = mybir.AxisListType

B, H, W, C = 8, 32, 32, 64
PAIRS = B // 2
HALVES = PAIRS // 2
L = H * W
P = 128
BLK = L // P
HB = 16
BANK = 512
D_STATE = 16
STEPS = 5
FRAME = (H + 2) * (W + 2)
GN_EPS, BN_EPS, LN_EPS = 1e-5, 1e-3, 1e-5
DT = 0.2

VEC = ["g_gamma", "g_beta", "g_mean", "g_var", "g1_gamma", "g1_beta", "g1_mean", "g1_var",
       "out_gamma", "out_beta", "out_mean", "out_var", "conv_bias", "ln_g", "ln_b", "proj_b",
       "m_conv_b", "m_dt_b", "m_D", "skip"]
V = {n: i for i, n in enumerate(VEC)}
V_WG = len(VEC)
V_CONVW = V_WG + 18
V_ALOG = V_CONVW + 4
NVEC = V_ALOG + D_STATE

MAT = ["ident", "neg_ident", "group_mean", "roll_up", "roll_down", "roll_diff", "dct"]
M = {n: i for i, n in enumerate(MAT)}


def fused_blocks(nc, x, vec, mats, conv_w, in_w, xbc_w, xdt_w, dtp_w, out_w, proj_w, out):
    ctx = ExitStack()
    with ctx:
        def sb(name, cols, dt=fp32, parts=P):
            return ctx.enter_context(nc.sbuf_tensor(name, [parts, cols], dt))

        sems = {}

        def S(name):
            if name not in sems:
                sems[name] = ctx.enter_context(nc.semaphore("s_" + name))
            return sems[name]

        xres = [sb(f"xres{k}", L) for k in range(2)]
        vecs = sb("vecs", NVEC + 32)
        mat = sb("mat", len(MAT) * P)
        convw = sb("convw", 9 * P)
        inw = sb("inw", 4 * C)
        xbcw = sb("xbcw", 96)
        dtw = sb("dtw", P)
        xdtw = sb("xdtw", P, parts=4)
        dtpw = sb("dtpw", P, parts=4)
        outw = sb("outw", C)
        projw = sb("projw", P)
        skipI = sb("skipI", P)
        diagD = sb("diagD", P)
        Amat = sb("Amat", D_STATE)
        par = sb("par", 16)
        cpow = sb("cpow", 16)
        diag = sb("diag", 18 * P)
        sel = ctx.enter_context(nc.sbuf_tensor("sel", [96, 32 * P], bf16))

        def mt(name):
            return mat[:, M[name] * P:(M[name] + 1) * P]

        def vc(name):
            return vecs[:, V[name]:V[name] + 1]

        ident = mt("ident")
        PS = [ctx.enter_context(nc.psum_tensor(f"ps{i}", [P, 2 * BANK], fp32)) for i in range(4)]

        ROWS34 = (H + 2) * W
        stage0 = [("fz", FRAME), ("fr", FRAME), ("hw", H * (W + 2)), ("X", ROWS34), ("Y", ROWS34)]
        stage0 += [(n, L) for n in ["XY", "sden", "R", "Dc", "Kx", "Ky", "g", "g1", "G", "G1", "Pmx", "Pmy", "P0", "Pe", "Sc"]]
        later = [("cfz", FRAME), ("X2", L), ("XNC", L), ("SZ", 2 * L), ("DL", 2 * L), ("DU", 2 * L), ("XS", 2 * L), ("BCS", L)]
        later += [(n, L) for n in ["XI", "AB", "EX", "UU", "LN", "RX", "R1"]] + [("MID", L // 2)]
        arena_cols = max(sum(n for _, n in stage0), sum(n for _, n in later))
        A, D = [], []
        for k in range(2):
            arena = sb(f"arena{k}", arena_cols)
            for parts, table in [(A, stage0), (D, later)]:
                t, at = {}, 0
                for name, cols in table:
                    t[name] = arena[:, at:at + cols]
                    at += cols
                parts.append(t)
            for t, names in [(A[k], [("st", 12), ("ag", 8), ("gn", 4), ("m", 16), ("v", 16), ("r", 16)])]:
                for name, cols in names:
                    t[name] = sb(f"{name}{k}", cols)
                    D[k][name] = t[name]
            d = D[k]
            d["BCS"] = d["BCS"].bitcast(bf16)
            d["MID"] = d["MID"].bitcast(bf16)
            d["N2"], d["XC"], d["SQ"], d["XN"] = d["XI"], d["AB"], d["EX"], d["UU"]
            d["V1"], d["N3"], d["T1"], d["A2"], d["T2"], d["X3"], d["OT"] = d["XC"], d["XI"], d["XC"], d["SQ"], d["XN"], d["LN"], d["RX"]
        DA, DB, HS = [D[0]["XI"], D[0]["AB"]], [D[0]["EX"], D[0]["UU"]], [D[0]["LN"], D[0]["RX"]]
        CB, HC = [D[1]["XI"], D[1]["AB"]], [D[1]["EX"], D[1]["UU"]]

        block = ctx.enter_context(nc.Block())

        def img(t):
            return t[:, 0:L].rearrange("p (h w) -> p h w", h=H)

        def frm(t):
            return t[:, 0:FRAME].rearrange("p (h w) -> p h w", h=H + 2)

        def wrapped(t):
            return t[:, :].rearrange("p (h w) -> p h w", h=H)

        def blk(t, k):
            return t[:, k * P:(k + 1) * P]

        def half(t, n):
            return t[:, n * BANK:(n + 1) * BANK]

        def dyn(t, b, n=None):
            return t[:, bass.ds(b * L, L)] if n is None else t[:, bass.ds(b * L + n * BANK, BANK)]

        def plain(eng):
            eng.sem_inc(S("waited"), 1)

        ONE = 1
        PRIMED = ["mix0", "mix1", "half_done", "scan0", "scan1", "hc0", "hc1", "dbu0", "dbu1",
                  "cb0", "cb1", "sum0", "sum1", "y_read"]

        x_pix = x.rearrange("b (k q) w c -> b (q w) k c", q=4)
        out_v = out.rearrange("b l (kb kq) c -> b kq l kb c", kq=4)

        @block.sync
        def _(sp):
            for name in PRIMED:
                sp.sem_inc(S(name), 1)
            sp.dma_start(vecs[:, :], vec).then_inc(S("vecs"), 16)
            sp.dma_start(mat[:, :], mats).then_inc(S("mats"), 16)
            for dst, src in [(convw, conv_w), (inw, in_w), (xbcw, xbc_w), (xdtw, xdt_w), (dtpw, dtp_w),
                             (outw, out_w), (projw, proj_w)]:
                sp.dma_start(dst[:, :], src).then_inc(S("weights"), 16)
            with sp.Fori(0, HALVES) as h:
                sp.wait_ge(S("half_done"), ONE + 2 * h)
                plain(sp)
                for k in range(2):
                    for b in range(2):
                        dst = A[k]["fr"][:, 0:L].rearrange("p (k b c) -> p b k c", b=2, c=C)[:, b]
                        sp.dma_start(dst, x_pix[4 * h + 2 * k + b]).then_inc(S(f"loaded{k}"), 16)
                for k in range(2):
                    sp.wait_ge(S("half_done"), ONE + 2 * h + k + 1)
                    plain(sp)
                    for b in range(2):
                        for kq in range(4):
                            src = D[k]["OT"][32 * kq:32 * kq + 32, :].rearrange("l (kb b c) -> l b kb c", b=2, c=C)[:, b]
                            sp.dma_start(out_v[4 * h + 2 * k + b][kq], src).then_inc(S("stored"), 16)
                sp.wait_ge(S("stored"), 256 * h + 256)
                plain(sp)

        @block.gpsimd
        def _(pool):
            tt = nc.gpsimd.tensor_tensor
            pool.memset(cpow[:, :], -0.5).then_inc(S("cpow"), 1)
            pool.wait_ge(S("cpow"), 1)
            pool.wait_ge(S("bn_var"), 3)
            tt(par[:, 6:9], par[:, 6:9], cpow[:, 0:3], ALU.pow).then_inc(S("bn_rstd"), 1)

            def root(t, wait, n, done):
                pool.wait_ge(S(wait), n)
                tt(t["gn"][:, 0:1], t["gn"][:, 0:1], cpow[:, 0:1], ALU.pow).then_inc(S(done), 1)

            def layer_root(t, n):
                pool.wait_ge(S("lvar"), n)
                tt(t["r"][:, :], t["v"][:, :], cpow[:, :], ALU.pow).then_inc(S("lrstd"), 1)

            for k in range(2):
                pool.memset(A[k]["fz"], 0.0).then_inc(S("frame_zero"), 1)
            with pool.Fori(0, HALVES) as h:
                for k in range(2):
                    root(A[k], "gvar", 8 * h + k + 1, "grstd")
                for k in range(2):
                    a = A[k]
                    pool.wait_ge(S("a_XYone"), 2 * h + k + 1)
                    tt(a["XY"][:, 0:L], a["X"][:, 0:L], a["Y"][:, 0:L], ALU.mult).then_inc(S("a_XY"), 1)
                for k in range(2):
                    a = A[k]
                    pool.wait_ge(S("a_D"), 2 * h + k + 1)
                    pool.wait_ge(S(f"a{k}_gg1"), 2 * h + 2)
                    tt(a["G1"][:, :], a["g1"][:, :], a["Dc"][:, :], ALU.mult).then_inc(S(f"a{k}_G"), 1)
                    tt(a["G"][:, :], a["g"][:, :], a["Dc"][:, :], ALU.mult).then_inc(S(f"a{k}_G"), 1)
                for k in range(2):
                    a = A[k]
                    pool.wait_ge(S("a_S"), 2 * h + k + 1)
                    pool.wait_ge(S(f"a{k}_G"), 2 * h + 2)
                    pool.wait_ge(S("a_div"), 2 * h + k + 1)
                    pool.wait_ge(S("a_Pe"), 2 * h + k + 1)
                    f_in = frm(a["fz"])[:, 1:33, 1:33]
                    tt(img(a["g"]), img(a["P0"]), f_in, ALU.mult).then_inc(S(f"a{k}_Wc"), 1)
                    pool.wait_ge(S(f"a{k}_Wc"), (STEPS + 1) * h + 1)
                    tt(a["G1"][:, :], a["g"][:, :], a["Sc"][:, :], ALU.add).then_inc(S(f"a{k}_U"), 1)
                with pool.Fori(0, STEPS) as t:
                    for k in range(2):
                        a = A[k]
                        pool.wait_ge(S(f"a{k}_h"), (STEPS + 1) * h + t + 1)
                        pool.wait_ge(S(f"mix{k}"), ONE + STEPS * h + t)
                        pool.wait_ge(S(f"a{k}_U"), (STEPS + 1) * h + t + 1)
                        hc = wrapped(a["hw"])[:, :, 1:33]
                        tt(img(a["X"]), img(a["Pe"]), hc, ALU.mult).then_inc(S(f"a{k}_e"), 1)
                        tt(img(a["g"]), img(a["P0"]), hc, ALU.mult).then_inc(S(f"a{k}_Wc"), 1)
                    for k in range(2):
                        a = A[k]
                        pool.wait_ge(S(f"a{k}_h"), (STEPS + 1) * h + t + 2)
                        pool.wait_ge(S(f"a{k}_Wc"), (STEPS + 1) * h + t + 2)
                        tt(a["G1"][:, :], a["g"][:, :], a["Sc"][:, :], ALU.add).then_inc(S(f"a{k}_U"), 1)
                for k in range(2):
                    a = A[k]
                    pool.wait_ge(S("a_bnout"), 2 * h + k + 1)
                    tt(xres[k][:, :], xres[k][:, :], a["X"][:, 0:L], ALU.add).then_inc(S("x1"), 1)
                for g in (1, 2):
                    for k in range(2):
                        root(D[k], "gvar", 8 * h + 2 * g + k + 1, "grstd")
                for k in range(2):
                    layer_root(D[k], 4 * h + k + 1)
                for b in range(2):
                    for k in range(2):
                        d = D[k]
                        i = 4 * h + 2 * b + k
                        pool.wait_ge(S("sp_parts"), i + 1)
                        tt(d["LN"], d["LN"], d["EX"], ALU.subtract).then_inc(S("sp_log"), 1)
                        pool.wait_ge(S("sp_log"), i + 1)
                        dl = d["DL"][:, b * L:b * L + L]
                        tt(dl, d["LN"], d["RX"], ALU.add).then_inc(S("delta"), 1)
                        pool.wait_ge(S("delta"), i + 1)
                        tt(d["DU"][:, b * L:b * L + L], dl, d["XS"][:, b * L:b * L + L], ALU.mult).then_inc(S("du"), 1)
                with pool.Fori(0, 2) as b:
                    for k in range(2):
                        with pool.Fori(0, D_STATE // 2) as n2:
                            for q in range(2):
                                m8 = (D_STATE // 2) * (4 * h + 2 * b + k) + n2
                                pool.wait_ge(S(f"scan{q}"), ONE + m8 + 1)
                                pool.wait_ge(S(f"cb{q}"), ONE + m8 + 1)
                                pool.wait_ge(S(f"sum{q}"), ONE + m8)
                                tt(HC[q], HS[q], CB[q], ALU.mult).then_inc(S(f"hc{q}"), 1)
                for k in range(2):
                    layer_root(D[k], 4 * h + 2 + k + 1)
                for k in range(2):
                    root(D[k], "gvar", 8 * h + 6 + k + 1, "grstd")

        @block.tensor
        def _(pe):
            mm = nc.tensor.matmul
            pe.wait_ge(S("mats"), 16)
            pe.wait_ge(S("weights"), 16 * 7)
            mm(PS[3][:, 0:P], xdtw[:, :], dtpw[:, :], start=True, stop=True).then_inc(S("dtw_ps"), 1)
            pe.wait_ge(S("dtw"), 1)
            pe.wait_ge(S("diag"), 18)

            def transposes(src, dst):
                for n in range(BLK):
                    last = nc.tensor.transpose(blk(dst, n), blk(src, n), ident)
                return last

            def group_mean(t, k, n):
                pe.wait_ge(S("stats"), n)
                mm(PS[2 * k + 1][:, 0:2], mt("group_mean"), t["ag"][:, 0:2], start=True, stop=True).then_inc(S("gmean"), 1)

            def conv3(ps, taps, frame):
                for n in range(2):
                    for tap in range(9):
                        dy, dx = tap // 3, tap % 3
                        last = mm(half(ps, n), taps(tap), frame[:, dy + HB * n:dy + HB * n + HB, dx:dx + W],
                                  start=(tap == 0), stop=(tap == 8))
                return last

            def project(ps, w, src):
                for n in range(2):
                    last = mm(half(ps, n)[0:w.shape[1], :], w, half(src, n), start=True, stop=True)
                return last

            with pe.Fori(0, HALVES) as h:
                for k in range(2):
                    pe.wait_ge(S(f"loaded{k}"), 32 * h + 32)
                    transposes(A[k]["fr"], PS[2 * k]).then_inc(S("a_xT"), 1)
                for k in range(2):
                    group_mean(A[k], k, 8 * h + k + 1)
                for w in range(2):
                    for k in range(2):
                        pe.wait_ge(S("a_fz"), 2 * h + k + 1)
                        pe.wait_ge(S("gvar"), 8 * h + k + 1)
                        conv3(PS[2 * k + 1 - w], lambda tap: blk(diag, 9 * (1 - w) + tap), frm(A[k]["fz"])).then_inc(S(f"a_conv{w}"), 1)
                for k in range(2):
                    a = A[k]
                    pe.wait_ge(S(f"a{k}_gg1"), 2 * h + 2)
                    g, ps = img(a["g"]), img(PS[2 * k])
                    for n in range(2):
                        r = slice(HB * n, HB * n + HB)
                        mm(ps[:, r, :], mt("roll_diff"), img(a["g1"])[:, r, :], start=True, stop=False)
                        mm(ps[:, r, 0:31], ident, g[:, r, 1:32], start=False, stop=False)
                        mm(ps[:, r, 31:32], ident, g[:, r, 0:1], start=False, stop=False)
                        mm(ps[:, r, 1:32], mt("neg_ident"), g[:, r, 0:31], start=False, stop=False)
                        last = mm(ps[:, r, 0:1], mt("neg_ident"), g[:, r, 31:32], start=False, stop=True)
                    last.then_inc(S("a_div"), 1)
                for k in range(2):
                    a = A[k]
                    pe.wait_ge(S("a_Pmy"), 2 * h + k + 1)
                    project(PS[2 * k + 1], mt("roll_down"), a["Pmy"]).then_inc(S("a_rollm"), 1)
                    pe.wait_ge(S("a_Ppy"), 2 * h + k + 1)
                    pe.wait_ge(S("a_Pe"), 2 * h + k + 1)
                    project(PS[2 * k], mt("roll_up"), a["R"]).then_inc(S("a_rollp"), 1)
                with pe.Fori(0, STEPS) as t:
                    for k in range(2):
                        a = A[k]
                        it = STEPS * h + t
                        for name, mname, src in [("c5", "roll_up", "Pmy"), ("c6", "roll_down", "sden"), ("e", "ident", "X"), ("ab", "ident", "R")]:
                            pe.wait_ge(S(f"a{k}_{name}"), it + 1)
                            if name == "c5":
                                pe.wait_ge(S("a_Q6"), 2 * h + k + 1)
                                pe.wait_ge(S(f"a{k}_h"), (STEPS + 1) * h + t + 1)
                            for n in range(2):
                                last = mm(half(PS[2 * k], n), mt(mname), half(a[src], n), start=(name == "c5"), stop=(name == "ab"))
                        last.then_inc(S(f"mix{k}"), 1)

                for k in range(2):
                    pe.wait_ge(S("x1"), 2 * h + k + 1)
                    group_mean(D[k], k, 8 * h + 2 + k + 1)
                for k in range(2):
                    pe.wait_ge(S("c_fz"), 2 * h + k + 1)
                    conv3(PS[2 * k], lambda tap: blk(convw, tap), frm(D[k]["cfz"])).then_inc(S("c_conv"), 1)
                for k in range(2):
                    group_mean(D[k], k, 8 * h + 4 + k + 1)
                for k in range(2):
                    pe.wait_ge(S("n2"), 2 * h + k + 1)
                    transposes(D[k]["N2"], PS[2 * k]).then_inc(S("n2T"), 1)
                for k in range(2):
                    pe.wait_ge(S("xn"), 2 * h + k + 1)
                    transposes(D[k]["XN"], PS[2 * k + 1]).then_inc(S("xnT"), 1)
                for b in range(2):
                    rows = slice(C * b, C * b + C)
                    for k in range(2):
                        d, i = D[k], 4 * h + 2 * b + k
                        if b == 0:
                            pe.wait_ge(S("xnc"), 2 * h + k + 1)
                        else:
                            pe.wait_ge(S("rx"), i - 1)
                            pe.wait_ge(S("r1"), i - 1)
                        for n in range(2):
                            last = mm(half(PS[2 * k], n), inw[rows, 0:P], half(d["XNC"], n)[rows, :], start=True, stop=True)
                        last.then_inc(S("xi"), 1)
                        for n in range(2):
                            last = mm(half(PS[2 * k + 1], n), inw[rows, P:2 * P], half(d["XNC"], n)[rows, :], start=True, stop=True)
                        last.then_inc(S("z"), 1)
                    for k in range(2):
                        d, i = D[k], 4 * h + 2 * b + k
                        xs = d["XS"][:, b * L:b * L + L]
                        pe.wait_ge(S("xs"), i + 1)
                        project(PS[2 * k], dtw[:, :], xs).then_inc(S("dt"), 1)
                        pe.wait_ge(S("sz"), i + 1)
                        project(PS[2 * k + 1], xbcw[:, :], xs).then_inc(S("bc"), 1)
                pe.wait_ge(S("r1"), 4 * h + 4)
                pe.wait_ge(S("rx"), 4 * h + 4)
                pe.wait_ge(S("bcs"), 4 * h + 4)
                plain(pe)
                with pe.Fori(0, 2) as b:
                    for k in range(2):
                        d = D[k]
                        i = 4 * h + 2 * b + k
                        base = (D_STATE // 2) * i
                        bcs = [d["BCS"][0:96, bass.ds(b * L + n * BANK, BANK)] for n in range(2)]

                        def rows_of(n2, q):
                            pe.wait_ge(S(f"dbu{q}"), ONE + base + n2)
                            for n in range(2):
                                last = mm(half(PS[q], n), sel[:, bass.ds((2 * n2 + q) * P, P)], bcs[n], start=True, stop=True)
                            last.then_inc(S(f"bb{q}"), 1)
                            pe.wait_ge(S(f"cb{1 - q}"), ONE + base + n2 + q)
                            for n in range(2):
                                last = mm(half(PS[2], n), sel[:, bass.ds((2 * n2 + q + D_STATE) * P, P)], bcs[n], start=True, stop=True)
                            last.then_inc(S(f"cps{q}"), 1)

                        def sum_of(n2, q):
                            pe.wait_ge(S(f"hc{q}"), ONE + base + n2 + 1)
                            for n in range(2):
                                last = mm(half(PS[3], n), ident, half(HC[q], n), start=False, stop=True, skip_group_check=True)
                            last.then_inc(S(f"sum{q}"), 1)

                        rows_of(0, 0)
                        rows_of(0, 1)
                        pe.wait_ge(S("y_read"), ONE + i)
                        for n in range(2):
                            mm(half(PS[3], n), diagD[:, :], dyn(d["XS"], b, n), start=True, stop=True, skip_group_check=True)
                        rows_of(1, 0)
                        with pe.Fori(0, D_STATE // 2 - 2) as n2:
                            sum_of(n2, 0)
                            rows_of(n2 + 1, 1)
                            sum_of(n2, 1)
                            rows_of(n2 + 2, 0)
                        last2 = D_STATE // 2 - 2
                        sum_of(last2, 0)
                        rows_of(last2 + 1, 1)
                        sum_of(last2, 1)
                        sum_of(last2 + 1, 0)
                        sum_of(last2 + 1, 1)
                pe.wait_ge(S("y_read"), ONE + 4 * h + 4)
                for k in range(2):
                    d = D[k]
                    for n in range(BLK):
                        mm(blk(PS[2 * k], n), blk(d["XNC"], n), skipI[:, :], start=(n % 4 == 0), stop=False, skip_group_check=True)
                    for n in range(BLK):
                        for b in range(2):
                            last = mm(blk(PS[2 * k], n)[:, C * b:C * b + C], blk(d["SZ"], BLK * b + n), outw[:, :],
                                      start=False, stop=True, skip_group_check=True)
                    last.then_inc(S("mo"), 1)
                for k in range(2):
                    pe.wait_ge(S("xn2"), 2 * h + k + 1)
                    transposes(D[k]["XN"], PS[2 * k + 1]).then_inc(S("xn2T"), 1)
                for k in range(2):
                    pe.wait_ge(S("v1"), 2 * h + k + 1)
                    project(PS[2 * k], projw[:, :], D[k]["V1"]).then_inc(S("proj"), 1)
                for k in range(2):
                    group_mean(D[k], k, 8 * h + 6 + k + 1)
                for k in range(2):
                    pe.wait_ge(S("n3"), 2 * h + k + 1)
                    transposes(D[k]["N3"], PS[2 * k]).then_inc(S("n3T"), 1)
                for k in range(2):
                    pe.wait_ge(S("t1"), 2 * h + k + 1)
                    for n in range(BLK):
                        last = mm(blk(PS[2 * k + 1], n), blk(D[k]["T1"], n), mt("dct"), start=True, stop=True, skip_group_check=True)
                    last.then_inc(S("dct1"), 1)
                for k in range(2):
                    pe.wait_ge(S("a2"), 2 * h + k + 1)
                    transposes(D[k]["A2"], PS[2 * k]).then_inc(S("a2T"), 1)
                for k in range(2):
                    d = D[k]
                    pe.wait_ge(S("t2"), 2 * h + k + 1)
                    for n in range(BLK):
                        if n % 4 == 0:
                            mm(half(PS[2 * k + 1], n // 4), mt("dct"), half(d["T2"], n // 4), start=True, stop=False, skip_group_check=True)
                        last = mm(blk(PS[2 * k + 1], n), blk(d["X3"], n), ident, start=False, stop=True, skip_group_check=True)
                    last.then_inc(S("final"), 1)

        @block.scalar
        def _(act):
            def av(out_, in_, func, scale=1.0, bias=0.0):
                return nc.scalar.activation(out_, in_, func, bias=bias, scale=scale)

            def gnorm(t, out_, in_, n):
                act.wait_ge(S("gshift"), n)
                return av(out_, in_, ACT.Identity, t["gn"][:, 0:1], t["gn"][:, 1:2])

            act.wait_ge(S("dtw_ps"), 1)
            av(dtw[:, :], PS[3][:, 0:P], ACT.Identity).then_inc(S("dtw"), 1)
            act.wait_ge(S("vecs"), 16)
            av(Amat[:, :], vecs[:, V_ALOG:V_ALOG + D_STATE], ACT.Exp).then_inc(S("Aexp"), 1)
            act.wait_ge(S("par"), 6)
            act.wait_ge(S("frame_zero"), 2)
            with act.Fori(0, HALVES) as h:
                for k in range(2):
                    act.wait_ge(S("a_xT"), 2 * h + k + 1)
                    av(xres[k][:, :], PS[2 * k][:, :], ACT.Identity).then_inc(S("a_x"), 1)
                for k in range(2):
                    a = A[k]
                    act.wait_ge(S("a_x"), 2 * h + k + 1)
                    gnorm(a, frm(a["fz"])[:, 1:33, 1:33], img(xres[k]), 8 * h + k + 1).then_inc(S("a_fz"), 1)
                for k in range(2):
                    a = A[k]
                    fr = frm(a["fr"])
                    gnorm(a, fr[:, 1:33, 1:33], img(xres[k]), 8 * h + k + 1).then_inc(S(f"a{k}_fri"), 1)
                    act.wait_ge(S(f"a{k}_fri"), 4 * h + 1)
                    av(fr[:, 1:33, 0:1], fr[:, 1:33, 2:3], ACT.Identity).then_inc(S(f"a{k}_fri"), 1)
                    av(fr[:, 1:33, 33:34], fr[:, 1:33, 31:32], ACT.Identity).then_inc(S(f"a{k}_fri"), 1)
                    act.wait_ge(S(f"a{k}_fri"), 4 * h + 3)
                    av(fr[:, 0:1, :], fr[:, 2:3, :], ACT.Identity)
                    av(fr[:, 33:34, :], fr[:, 31:32, :], ACT.Identity).then_inc(S(f"a{k}_fri"), 1)
                    gnorm(a, wrapped(a["hw"])[:, :, 1:33], img(xres[k]), 8 * h + k + 1).then_inc(S(f"a{k}_h"), 1)
                for k in range(2):
                    a = A[k]
                    act.wait_ge(S("a_sobel"), 2 * h + k + 1)
                    av(a["Dc"][:, 0:L], a["R"][:, 0:L], ACT.Square, 0.5).then_inc(S(f"a{k}_sq"), 1)
                    av(a["Kx"][:, 0:L], a["XY"][:, 0:L], ACT.Square, 0.5).then_inc(S(f"a{k}_sq"), 1)
                    act.wait_ge(S(f"a{k}_sq"), 2 * h + 2)
                    av(a["X"][:, 0:L], a["Dc"][:, 0:L], ACT.Identity, 1.0, 1.0)
                    av(a["Y"][:, 0:L], a["Kx"][:, 0:L], ACT.Identity, 1.0, 1.0).then_inc(S("a_XYone"), 1)
                for k in range(2):
                    act.wait_ge(S("a_conv0"), 2 * h + k + 1)
                    av(A[k]["g1"][:, :], PS[2 * k + 1][:, :], ACT.Relu, par[:, 2:3], par[:, 3:4]).then_inc(S(f"a{k}_gg1"), 1)
                for k in range(2):
                    act.wait_ge(S("a_conv1"), 2 * h + k + 1)
                    av(A[k]["g"][:, :], PS[2 * k][:, :], ACT.Relu, par[:, 0:1], par[:, 1:2]).then_inc(S(f"a{k}_gg1"), 1)
                for k in range(2):
                    a = A[k]
                    act.wait_ge(S("a_rollm"), 2 * h + k + 1)
                    act.wait_ge(S("a_Pm"), 2 * h + k + 1)
                    av(a["Kx"][:, :], PS[2 * k + 1][:, :], ACT.Identity).then_inc(S("a_Q5"), 1)
                    act.wait_ge(S("a_rollp"), 2 * h + k + 1)
                    av(a["Ky"][:, :], PS[2 * k][:, :], ACT.Identity).then_inc(S("a_Q6"), 1)
                with act.Fori(0, STEPS) as t:
                    for k in range(2):
                        hw = wrapped(A[k]["hw"])
                        act.wait_ge(S(f"a{k}_h"), (STEPS + 1) * h + t + 1)
                        av(hw[:, :, 0:1], hw[:, :, 32:33], ACT.Identity)
                        av(hw[:, :, 33:34], hw[:, :, 1:2], ACT.Identity).then_inc(S(f"a{k}_wrap"), 1)
                for k in range(2):
                    a = A[k]
                    act.wait_ge(S(f"a{k}_h"), (STEPS + 1) * h + STEPS + 1)
                    av(img(a["X"]), wrapped(a["hw"])[:, :, 1:33], ACT.Relu, par[:, 4:5], par[:, 5:6]).then_inc(S("a_bnout"), 1)

                for k in range(2):
                    gnorm(D[k], frm(D[k]["cfz"])[:, 1:33, 1:33], img(xres[k]), 8 * h + 2 + k + 1).then_inc(S("c_fz"), 1)
                for k in range(2):
                    gnorm(D[k], D[k]["N2"], D[k]["X2"], 8 * h + 4 + k + 1).then_inc(S("n2"), 1)
                for k in range(2):
                    act.wait_ge(S("xc"), 4 * h + k + 1)
                    av(D[k]["SQ"], D[k]["XC"], ACT.Square).then_inc(S("csq"), 1)
                for k in range(2):
                    act.wait_ge(S("xnT"), 2 * h + k + 1)
                    av(D[k]["XNC"], PS[2 * k + 1][:, :], ACT.Identity, vc("ln_g"), vc("ln_b")).then_inc(S("xnc"), 1)
                for b in range(2):
                    cols = slice(b * L, b * L + L)
                    for k in range(2):
                        i = 4 * h + 2 * b + k
                        act.wait_ge(S("z"), i + 1)
                        av(D[k]["SZ"][:, cols], PS[2 * k + 1][:, :], ACT.Silu).then_inc(S("sz"), 1)
                    for k in range(2):
                        i = 4 * h + 2 * b + k
                        act.wait_ge(S("cconv"), i + 1)
                        av(D[k]["XS"][:, cols], D[k]["XI"], ACT.Silu, 1.0, vc("m_conv_b")).then_inc(S("xs"), 1)
                    for k in range(2):
                        d, i = D[k], 4 * h + 2 * b + k
                        act.wait_ge(S("bc"), i + 1)
                        av(d["BCS"][0:96, cols], PS[2 * k + 1][0:96, :], ACT.Identity).then_inc(S("bc_read"), 1)
                    for k in range(2):
                        d, i = D[k], 4 * h + 2 * b + k
                        act.wait_ge(S("dt"), i + 1)
                        av(d["AB"], PS[2 * k][:, :], ACT.Abs, 1.0, vc("m_dt_b")).then_inc(S("dtread"), 1)
                    for k in range(2):
                        d, i = D[k], 4 * h + 2 * b + k
                        act.wait_ge(S("dtread"), i + 1)
                        if b == 1:
                            act.wait_ge(S("delta"), i - 1)
                        av(d["EX"], d["AB"], ACT.Exp, -1.0).then_inc(S("ex"), 1)
                        act.wait_ge(S("ex"), i + 1)
                        av(d["UU"], d["EX"], ACT.Identity, 1.0, 1.0).then_inc(S("uu"), 1)
                        act.wait_ge(S("uu"), i + 1)
                        av(d["LN"], d["UU"], ACT.Ln).then_inc(S("ln"), 1)
                    for k in range(2):
                        d, i = D[k], 4 * h + 2 * b + k
                        act.wait_ge(S("r1"), i + 1)
                        av(d["MID"][0:96, :], d["R1"][0:96, :], ACT.Identity).then_inc(S("mid"), 1)
                        av(d["BCS"][32:64, cols], d["R1"][32:64, :], ACT.Identity).then_inc(S("mid"), 1)
                act.wait_ge(S("delta"), 4 * h + 4)
                act.wait_ge(S("du"), 4 * h + 4)
                act.wait_ge(S("bcs"), 4 * h + 4)
                plain(act)
                with act.Fori(0, 2) as b:
                    for k in range(2):
                        d = D[k]
                        base = (D_STATE // 2) * (4 * h + 2 * b + k)

                        def decay(n2, q):
                            act.wait_ge(S(f"scan{q}"), ONE + base + n2)
                            plain(act)
                            av(DA[q], dyn(d["DL"], b), ACT.Exp, Amat[:, bass.ds(2 * n2 + q, 1)]).then_inc(S(f"da{q}"), 1)

                        def copy_c(n2, q):
                            act.wait_ge(S(f"cps{q}"), base + n2 + 1)
                            act.wait_ge(S(f"hc{q}"), ONE + base + n2)
                            av(CB[q], PS[2][:, :], ACT.Identity).then_inc(S(f"cb{q}"), 1)

                        decay(0, 0)
                        decay(0, 1)
                        with act.Fori(0, D_STATE // 2 - 1) as n2:
                            for q in range(2):
                                copy_c(n2, q)
                                decay(n2 + 1, q)
                        for q in range(2):
                            copy_c(D_STATE // 2 - 1, q)
                for k in range(2):
                    act.wait_ge(S("xc"), 4 * h + 2 + k + 1)
                    av(D[k]["SQ"], D[k]["XC"], ACT.Square).then_inc(S("csq"), 1)
                for k in range(2):
                    act.wait_ge(S("xn2T"), 2 * h + k + 1)
                    av(D[k]["V1"], PS[2 * k + 1][:, :], ACT.Identity, vc("ln_g"), vc("ln_b")).then_inc(S("v1"), 1)
                for k in range(2):
                    gnorm(D[k], D[k]["N3"], D[k]["X3"], 8 * h + 6 + k + 1).then_inc(S("n3"), 1)
                for k in range(2):
                    act.wait_ge(S("n3T"), 2 * h + k + 1)
                    av(D[k]["T1"], PS[2 * k][:, :], ACT.Identity).then_inc(S("t1"), 1)
                for k in range(2):
                    act.wait_ge(S("dct1"), 2 * h + k + 1)
                    av(D[k]["A2"].rearrange("p (k w) -> p w k", k=H), PS[2 * k + 1][:, :].rearrange("p (w k) -> p w k", w=W), ACT.Identity).then_inc(S("a2"), 1)
                for k in range(2):
                    act.wait_ge(S("a2T"), 2 * h + k + 1)
                    av(D[k]["T2"], PS[2 * k][:, :], ACT.Identity).then_inc(S("t2"), 1)
                for k in range(2):
                    act.wait_ge(S("final"), 2 * h + k + 1)
                    av(D[k]["OT"], PS[2 * k + 1][:, :], ACT.Identity).then_inc(S("half_done"), 1)

        @block.vector
        def _(dve):
            tt = nc.vector.tensor_tensor
            stt = nc.vector.scalar_tensor_tensor
            ts = nc.vector.tensor_scalar
            chain = [0]

            def link(ins):
                chain[0] += 1
                ins.then_inc(S("setup_step"), 1)
                dve.wait_ge(S("setup_step"), chain[0])

            dve.wait_ge(S("vecs"), 16)
            for n, name in enumerate(["g", "g1", "out"]):
                ts(par[:, 6 + n:7 + n], vc(name + "_var"), BN_EPS, None, ALU.add).then_inc(S("bn_var"), 1)
            dve.wait_ge(S("mats"), 16)
            for t in range(18):
                ts(blk(diag, t), ident, vecs[:, V_WG + t:V_WG + t + 1], None, ALU.mult).then_inc(S("diag"), 1)
            ts(skipI[:, :], ident, vc("skip"), None, ALU.mult)
            ts(diagD[:, :], ident, vc("m_D"), None, ALU.mult)
            nc.vector.tensor_copy(sel[:, :].rearrange("k (j m) -> k j m", m=P),
                                  vecs[0:96, NVEC:NVEC + 32].unsqueeze(2).to_broadcast([96, 32, P])).then_inc(S("diag"), 1)
            dve.wait_ge(S("Aexp"), 1)
            link(ts(Amat[:, :], Amat[:, :], -1.0, None, ALU.mult))
            dve.wait_ge(S("bn_rstd"), 1)
            for n, (name, f) in enumerate([("g", DT), ("g1", DT), ("out", 1.0)]):
                link(stt(par[:, 9:10], vc(name + "_gamma"), f, par[:, 6 + n:7 + n], ALU.mult, ALU.mult))
                link(tt(par[:, 10:11], vc(name + "_mean"), par[:, 9:10], ALU.mult))
                ts(par[:, 2 * n:2 * n + 1], par[:, 9:10], 1.0, None, ALU.mult).then_inc(S("par"), 1)
                stt(par[:, 2 * n + 1:2 * n + 2], vc(name + "_beta"), f, par[:, 10:11], ALU.mult, ALU.subtract).then_inc(S("par"), 1)
                dve.wait_ge(S("par"), 2 * n + 2)

            def stats(src, t, h, g, k):
                step, n0 = S(f"gstep{k}"), 20 * h + 5 * g
                nc.vector.bn_stats(t["st"][:, 0:6], half(src, 0)).then_inc(step, 1)
                nc.vector.bn_stats(t["st"][:, 6:12], half(src, 1)).then_inc(step, 1)
                dve.wait_ge(step, n0 + 2)
                plain(dve)
                nc.vector.bn_aggr(t["ag"][:, 0:2], t["st"][:, :]).then_inc(step, 1)
                dve.wait_ge(step, n0 + 3)
                stt(t["ag"][:, 1:2], t["ag"][:, 0:1], t["ag"][:, 0:1], t["ag"][:, 1:2], ALU.mult, ALU.add).then_inc(S("stats"), 1)

            def group_var(t, h, g, k):
                step, n0, n = S(f"gstep{k}"), 20 * h + 5 * g + 3, 8 * h + 2 * g + k + 1
                dve.wait_ge(S("gmean"), n)
                ts(t["ag"][:, 2:4], PS[2 * k + 1][:, 0:2], 1.0, None, ALU.mult).then_inc(step, 1)
                dve.wait_ge(step, n0 + 1)
                stt(t["ag"][:, 4:5], t["ag"][:, 2:3], t["ag"][:, 2:3], t["ag"][:, 3:4], ALU.mult, ALU.subtract).then_inc(step, 1)
                dve.wait_ge(step, n0 + 2)
                ts(t["gn"][:, 0:1], t["ag"][:, 4:5], -1.0, GN_EPS, ALU.mult, ALU.add).then_inc(S("gvar"), 1)

            def group_shift(t, h, g, k):
                dve.wait_ge(S("grstd"), 8 * h + 2 * g + k + 1)
                stt(t["gn"][:, 1:2], t["ag"][:, 2:3], -1.0, t["gn"][:, 0:1], ALU.mult, ALU.mult).then_inc(S("gshift"), 1)

            def group_norms(ts_, h, g):
                for k in range(2):
                    group_var(ts_[k], h, g, k)
                for k in range(2):
                    group_shift(ts_[k], h, g, k)

            def layer_norms(ps, h, g, done):
                def v3(t):
                    return t[:, :].rearrange("p (g c) -> p g c", c=C)

                for k in range(2):
                    d, step, n0 = D[k], S(f"lstep{k}"), 6 * h + 3 * g
                    dve.wait_ge(S(["n2T", "mo"][g]), 2 * h + k + 1)
                    nc.vector.reduce_sum(d["m"][:, :], v3(ps[k]), axis=AX.X).then_inc(step, 1)
                    dve.wait_ge(step, n0 + 1)
                    ts(d["m"][:, :], d["m"][:, :], 1.0 / C, None, ALU.mult).then_inc(step, 1)
                    dve.wait_ge(step, n0 + 2)
                    tt(v3(d["XC"]), v3(ps[k]), d["m"][:, :].unsqueeze(2).to_broadcast([P, 16, C]), ALU.subtract).then_inc(S("xc"), 1)
                for k in range(2):
                    d, step, n0 = D[k], S(f"lstep{k}"), 6 * h + 3 * g
                    dve.wait_ge(S("csq"), 4 * h + 2 * g + k + 1)
                    nc.vector.reduce_sum(d["v"][:, :], v3(d["SQ"]), axis=AX.X).then_inc(step, 1)
                    dve.wait_ge(step, n0 + 3)
                    ts(d["v"][:, :], d["v"][:, :], 1.0 / C, LN_EPS, ALU.mult, ALU.add).then_inc(S("lvar"), 1)
                for k in range(2):
                    d = D[k]
                    dve.wait_ge(S("lrstd"), 4 * h + 2 * g + k + 1)
                    tt(v3(d["XN"]), v3(d["XC"]), d["r"][:, :].unsqueeze(2).to_broadcast([P, 16, C]), ALU.mult).then_inc(S(done), 1)

            with dve.Fori(0, HALVES) as h:
                for k in range(2):
                    dve.wait_ge(S("a_x"), 2 * h + k + 1)
                    stats(xres[k], A[k], h, 0, k)
                group_norms(A, h, 0)
                for k in range(2):
                    a = A[k]
                    fr = frm(a["fr"])
                    X = a["X"].rearrange("p (h w) -> p h w", w=W)
                    Y = a["Y"].rearrange("p (h w) -> p h w", w=W)
                    sob = S(f"a{k}_sob")
                    dve.wait_ge(S(f"a{k}_fri"), 4 * h + 4)
                    tt(X, fr[:, :, 0:32], fr[:, :, 2:34], ALU.add).then_inc(sob, 1)
                    tt(Y, fr[:, :, 2:34], fr[:, :, 0:32], ALU.subtract).then_inc(sob, 1)
                    dve.wait_ge(sob, 4 * h + 1)
                    stt(X, fr[:, :, 1:33], 2.0, X, ALU.mult, ALU.add).then_inc(sob, 1)
                    dve.wait_ge(sob, 4 * h + 2)
                    tt(img(a["XY"]), Y[:, 0:32, :], Y[:, 2:34, :], ALU.add).then_inc(sob, 1)
                    dve.wait_ge(sob, 4 * h + 3)
                    tt(img(a["R"]), X[:, 2:34, :], X[:, 0:32, :], ALU.subtract)
                    dve.wait_ge(sob, 4 * h + 4)
                    stt(img(a["XY"]), Y[:, 1:33, :], 2.0, img(a["XY"]), ALU.mult, ALU.add).then_inc(S("a_sobel"), 1)

                def coef_steps(k, first):
                    a, n0, done = A[k], 5 * h, S(f"a{k}_coef")
                    n = 2 * h + k + 1
                    if first:
                        dve.wait_ge(S("a_XYone"), n)
                        tt(a["sden"], a["X"][:, 0:L], a["Y"][:, 0:L], ALU.add).then_inc(done, 1)
                        dve.wait_ge(S("a_XY"), n)
                        dve.wait_ge(done, n0 + 1)
                        stt(a["sden"], a["sden"], 2 * DT, a["XY"], ALU.mult, ALU.add).then_inc(done, 1)
                        dve.wait_ge(done, n0 + 2)
                        nc.vector.reciprocal(a["R"], a["sden"]).then_inc(done, 1)
                        dve.wait_ge(done, n0 + 3)
                        tt(a["Dc"], a["XY"], a["R"], ALU.mult).then_inc(S("a_D"), 1)
                        stt(a["Kx"], a["Y"][:, 0:L], 2 * DT, a["R"], ALU.mult, ALU.mult)
                        stt(a["Ky"], a["X"][:, 0:L], 2 * DT, a["R"], ALU.mult, ALU.mult).then_inc(done, 1)
                        dve.wait_ge(done, n0 + 4)
                        tt(a["P0"], a["Kx"], a["Ky"], ALU.add).then_inc(done, 1)
                        dve.wait_ge(S("a_D"), n)
                        dve.wait_ge(done, n0 + 5)
                        tt(a["P0"], a["Dc"], a["P0"], ALU.subtract)
                        stt(img(a["Sc"]), frm(a["fz"])[:, 1:33, 1:33], 2 * DT, img(a["Dc"]), ALU.mult, ALU.mult).then_inc(S("a_S"), 1)
                    else:
                        dve.wait_ge(S(f"a{k}_G"), 2 * h + 1)
                        tt(a["Pmy"], a["Ky"], a["G1"], ALU.subtract).then_inc(S("a_Pmy"), 1)
                        tt(a["R"], a["Ky"], a["G1"], ALU.add).then_inc(S("a_Ppy"), 1)
                        dve.wait_ge(S("a_div"), n)
                        tt(a["Pe"], a["Dc"], PS[2 * k][:, :], ALU.mult).then_inc(S("a_Pe"), 1)
                        dve.wait_ge(S(f"a{k}_G"), 2 * h + 2)
                        tt(a["Pmx"], a["Kx"], a["G"], ALU.subtract)
                        tt(a["G"], a["Kx"], a["G"], ALU.add).then_inc(S("a_Pm"), 1)
                for first in (True, False):
                    for k in range(2):
                        coef_steps(k, first)
                with dve.Fori(0, STEPS) as t:
                    it = STEPS * h + t
                    for k in range(2):
                        a = A[k]
                        hw = wrapped(a["hw"])
                        hc = hw[:, :, 1:33]
                        dve.wait_ge(S("a_Q6"), 2 * h + k + 1)
                        dve.wait_ge(S(f"mix{k}"), ONE + it)
                        dve.wait_ge(S(f"a{k}_h"), (STEPS + 1) * h + t + 1)
                        tt(img(a["Pmy"]), img(a["Kx"]), hc, ALU.mult).then_inc(S(f"a{k}_c5"), 1)
                        tt(img(a["sden"]), img(a["Ky"]), hc, ALU.mult).then_inc(S(f"a{k}_c6"), 1)
                        dve.wait_ge(S(f"a{k}_wrap"), it + 1)
                        tt(img(a["R"]), img(a["Pmx"]), hw[:, :, 0:32], ALU.mult)
                        tt(img(a["XY"]), img(a["G"]), hw[:, :, 2:34], ALU.mult).then_inc(S(f"a{k}_abm"), 1)
                        dve.wait_ge(S(f"a{k}_abm"), it + 1)
                        tt(a["R"], a["R"], a["XY"], ALU.add).then_inc(S(f"a{k}_ab"), 1)
                    for k in range(2):
                        a = A[k]
                        dve.wait_ge(S(f"mix{k}"), ONE + it + 1)
                        dve.wait_ge(S(f"a{k}_U"), (STEPS + 1) * h + t + 1)
                        dve.wait_ge(S(f"a{k}_Wc"), (STEPS + 1) * h + t + 2)
                        tt(wrapped(a["hw"])[:, :, 1:33], img(PS[2 * k]), img(a["G1"]), ALU.add).then_inc(S(f"a{k}_h"), 1)

                for k in range(2):
                    dve.wait_ge(S("x1"), 2 * h + k + 1)
                    stats(xres[k], D[k], h, 1, k)
                group_norms(D, h, 1)
                for k in range(2):
                    dve.wait_ge(S("c_conv"), 2 * h + k + 1)
                    stt(D[k]["X2"], PS[2 * k][:, :], vc("conv_bias"), xres[k][:, :], ALU.add, ALU.add).then_inc(S("X2"), 1)
                    dve.wait_ge(S("X2"), 2 * h + k + 1)
                    stats(D[k]["X2"], D[k], h, 2, k)
                group_norms(D, h, 2)
                layer_norms([PS[0], PS[2]], h, 0, "xn")
                for b in range(2):
                    cols = slice(b * L, b * L + L)
                    for k in range(2):
                        d, i = D[k], 4 * h + 2 * b + k
                        dve.wait_ge(S("xi"), i + 1)
                        if b == 1:
                            dve.wait_ge(S("xs"), i - 1)
                        w = [vecs[:, V_CONVW + t:V_CONVW + t + 1] for t in range(4)]
                        ts(d["XI"], PS[2 * k][:, :], w[3], None, ALU.mult).then_inc(S("cstep"), 1)
                        for t in range(1, 4):
                            dve.wait_ge(S("cstep"), 3 * i + t)
                            stt(d["XI"][:, t:L], PS[2 * k][:, 0:L - t], w[3 - t], d["XI"][:, t:L], ALU.mult, ALU.add)\
                                .then_inc(S("cstep") if t < 3 else S("cconv"), 1)
                    for k in range(2):
                        d, i = D[k], 4 * h + 2 * b + k
                        dve.wait_ge(S("bc_read"), i + 1)
                        tt(d["R1"][0:96, :], PS[2 * k + 1][0:96, :], d["BCS"][0:96, cols], ALU.subtract).then_inc(S("r1"), 1)
                    for k in range(2):
                        d, i = D[k], 4 * h + 2 * b + k
                        dve.wait_ge(S("dtread"), i + 1)
                        if b == 1:
                            dve.wait_ge(S("delta"), i - 1)
                        ts(d["RX"], PS[2 * k][:, :], vc("m_dt_b"), 0.0, ALU.add, ALU.max).then_inc(S("rx"), 1)
                    for k in range(2):
                        d, i = D[k], 4 * h + 2 * b + k
                        dve.wait_ge(S("ln"), i + 1)
                        stt(d["EX"], d["UU"], -1.0, d["EX"], ALU.add, ALU.subtract).then_inc(S("sp_parts"), 1)
                        dve.wait_ge(S("mid"), 2 * i + 2)
                        dve.wait_ge(S("r1"), i + 1)
                        tt(d["BCS"][64:96, cols], d["R1"][64:96, :], d["MID"][64:96, :], ALU.subtract).then_inc(S("bcs"), 1)
                dve.wait_ge(S("du"), 4 * h + 4)
                plain(dve)
                with dve.Fori(0, 2) as b:
                    for k in range(2):
                        d = D[k]
                        i = 4 * h + 2 * b + k
                        with dve.Fori(0, D_STATE // 2) as n2:
                            for q in range(2):
                                m8 = (D_STATE // 2) * i + n2
                                dve.wait_ge(S(f"bb{q}"), m8 + 1)
                                dve.wait_ge(S(f"scan{q}"), ONE + m8)
                                tt(DB[q], dyn(d["DU"], b), PS[q][:, :], ALU.mult).then_inc(S(f"dbu{q}"), 1)
                                dve.wait_ge(S(f"da{q}"), m8 + 1)
                                dve.wait_ge(S(f"dbu{q}"), ONE + m8 + 1)
                                dve.wait_ge(S(f"hc{q}"), ONE + m8)
                                nc.vector.tensor_tensor_scan(HS[q], DA[q], DB[q], 0.0, ALU.mult, ALU.add).then_inc(S(f"scan{q}"), 1)
                        dve.wait_ge(S("sum1"), ONE + (D_STATE // 2) * (i + 1))
                        tt(dyn(d["SZ"], b), PS[3][:, :], dyn(d["SZ"], b), ALU.mult).then_inc(S("y_read"), 1)
                layer_norms([PS[0], PS[2]], h, 1, "xn2")
                for k in range(2):
                    d = D[k]
                    dve.wait_ge(S("proj"), 2 * h + k + 1)
                    stt(d["X3"].rearrange("p (w h) -> p h w", w=W), img(PS[2 * k]), vc("proj_b"), img(d["X2"]), ALU.add, ALU.add).then_inc(S("X3"), 1)
                    dve.wait_ge(S("X3"), 2 * h + k + 1)
                    stats(d["X3"], d, h, 3, k)
                group_norms(D, h, 3)


def kernel(**inputs):
    import numpy as np
    import concourse.bacc as bacc
    from concourse.bass_utils import run_bass_kernel_spmd

    v = {k: np.asarray(a) for k, a in inputs.items()}

    def two(a):
        return np.concatenate([a, a], axis=0)

    cols = []
    for n in VEC:
        if n[0] in "go" and n != "skip":
            cols.append(two(v["L0_conv_" + n]))
        elif n == "conv_bias":
            cols.append(two(v["L1_conv_bias"]))
        elif n in ("ln_g", "ln_b", "proj_b"):
            cols.append(two(v["L2_conv_" + n]))
        elif n == "m_conv_b":
            cols.append(v["L2_conv_conv_b"])
        elif n == "m_dt_b":
            cols.append(v["L2_conv_dt_proj_b"])
        elif n == "m_D":
            cols.append(v["L2_conv_D"])
        else:
            cols.append(np.broadcast_to(v["L2_conv_skip_scale"], (P,)))
    wg = v["L0_conv_wg"].reshape(9, C).T
    wg1 = v["L0_conv_wg1"].reshape(9, C).T
    row32 = np.zeros((P, 32), np.float32)
    row32[np.arange(P), np.arange(P) % 32] = 1.0
    vec = np.concatenate([np.stack(cols, axis=1), two(wg), two(wg1), v["L2_conv_conv_w"], v["L2_conv_A_log"], row32], axis=1)

    r = np.arange(P)
    eye = np.eye(P, dtype=np.float32)
    group = (r[:, None] // 2 == r[None, :] // 2).astype(np.float32) * np.float32(0.5)
    prev = (r // C) * C + (r % C - 1) % C
    nxt = (r // C) * C + (r % C + 1) % C
    up = np.zeros((P, P), np.float32)
    up[prev, r] = 1.0
    down = np.zeros((P, P), np.float32)
    down[nxt, r] = 1.0
    n = np.arange(H)
    m = np.cos(np.pi * (n[None, :] + 0.5) * n[:, None] / H) * np.sqrt(2.0 / H)
    m[0] *= 1.0 / np.sqrt(2.0)
    dct = np.zeros((P, P), np.float32)
    for q in range(4):
        dct[q * H:(q + 1) * H, q * H:(q + 1) * H] = m.T
    mats = np.concatenate([eye, -eye, group, up, down, down - up, dct], axis=1).astype(np.float32)

    conv = v["L1_conv_kernel"].reshape(9, C, C)
    conv_w = np.zeros((P, 9, P), np.float32)
    proj_w = np.zeros((P, P), np.float32)
    for b in range(2):
        s = slice(b * C, b * C + C)
        conv_w[s, :, s] = conv.transpose(1, 0, 2)
        proj_w[s, s] = v["L2_conv_proj_w"].T
    in_w = two(v["L2_conv_in_proj_w"].T)
    xw = v["L2_conv_x_proj_w"]
    xbc_w = np.concatenate([xw[4:].T] * 3, axis=1)

    arrays = {"x": v["x"], "vec": vec, "mats": mats, "conv_w": conv_w.reshape(P, 9 * P), "in_w": in_w,
              "xbc_w": xbc_w, "xdt_w": xw[:4], "dtp_w": v["L2_conv_dt_proj_w"].T,
              "out_w": v["L2_conv_out_proj_w"].T, "proj_w": proj_w}
    arrays = {k: np.ascontiguousarray(a) for k, a in arrays.items()}

    nc = bacc.Bacc("TRN2", target_bir_lowering=False, num_devices=1)
    args = [nc.dram_tensor(k, a.shape, mybir.dt.from_np(a.dtype), kind="ExternalInput").ap() for k, a in arrays.items()]
    out = nc.dram_tensor("out", (B, H, W, C), fp32, kind="ExternalOutput").ap()
    fused_blocks(nc, *args, out)
    res = run_bass_kernel_spmd(nc, [arrays], core_ids=[0])
    return res.results[0]["out"]
```

```python
import concourse.bass as bass
from concourse import mybir
from contextlib import ExitStack

fp32 = mybir.dt.float32
bf16 = mybir.dt.bfloat16
ALU = mybir.AluOpType
ACT = mybir.ActivationFunctionType
AX = mybir.AxisListType

B, H, W, C = 8, 32, 32, 64
PAIRS = B // 2
HALVES = PAIRS // 2
L = H * W
P = 128
BLK = L // P
HB = 16
BANK = 512
D_STATE = 16
STEPS = 5
OFF_PE = 3
PE_TAPS = [9 * w + tap for w in range(2) for tap in range(OFF_PE, 9)]
FRAME = (H + 2) * (W + 2)
GN_EPS, BN_EPS, LN_EPS = 1e-5, 1e-3, 1e-5
DT = 0.2

VEC = ["g_gamma", "g_beta", "g_mean", "g_var", "g1_gamma", "g1_beta", "g1_mean", "g1_var",
       "out_gamma", "out_beta", "out_mean", "out_var", "conv_bias", "ln_g", "ln_b", "proj_b",
       "m_conv_b", "m_dt_b", "m_D", "skip"]
V = {n: i for i, n in enumerate(VEC)}
V_WG = len(VEC)
V_CONVW = V_WG + 18
V_ALOG = V_CONVW + 4
NVEC = V_ALOG + D_STATE

MAT = ["ident", "neg_ident", "group_mean", "roll_up", "roll_down", "roll_diff", "dct"]
M = {n: i for i, n in enumerate(MAT)}


def fused_blocks(nc, x, vec, mats, conv_w, in_w, xbc_w, xdt_w, dtp_w, out_w, proj_w, out):
    ctx = ExitStack()
    with ctx:
        def sb(name, cols, dt=fp32, parts=P):
            return ctx.enter_context(nc.sbuf_tensor(name, [parts, cols], dt))

        sems = {}

        def S(name):
            if name not in sems:
                sems[name] = ctx.enter_context(nc.semaphore("s_" + name))
            return sems[name]

        xres = [sb(f"xres{k}", L) for k in range(2)]
        vecs = sb("vecs", NVEC + 32)
        mat = sb("mat", len(MAT) * P)
        convw = sb("convw", 9 * P)
        inw = sb("inw", 8 * C)
        xbcw = sb("xbcw", 96)
        dtw = sb("dtw", P)
        xdtw = sb("xdtw", P, parts=4)
        dtpw = sb("dtpw", P, parts=4)
        outw = sb("outw", C)
        projw = sb("projw", P)
        skipI = sb("skipI", P)
        diagD = sb("diagD", P)
        Amat = sb("Amat", D_STATE)
        par = sb("par", 16)
        cpow = sb("cpow", 16)
        diag = sb("diag", 18 * P)
        sel = ctx.enter_context(nc.sbuf_tensor("sel", [96, 32 * P], bf16))

        def mt(name):
            return mat[:, M[name] * P:(M[name] + 1) * P]

        def vc(name):
            return vecs[:, V[name]:V[name] + 1]

        ident = mt("ident")
        PS = [ctx.enter_context(nc.psum_tensor(f"ps{i}", [P, 2 * BANK], fp32)) for i in range(4)]

        ROWS34 = (H + 2) * W
        stage0 = [("fz", FRAME), ("fr", FRAME), ("hw", H * (W + 2)), ("X", ROWS34), ("Y", ROWS34)]
        stage0 += [(n, L) for n in ["XY", "sden", "R", "Dc", "Kx", "Ky", "g", "g1", "G", "G1", "Pmx", "Pmy", "P0", "Pe", "Sc"]]
        later = [("cfz", FRAME), ("X2", L), ("XNC", L), ("SZ", 2 * L), ("DL", 2 * L), ("DU", 2 * L), ("XS", 2 * L), ("BCS", L)]
        later += [(n, L) for n in ["W0", "W1", "W2", "W3", "W4", "W5", "R1"]] + [("HI", L // 2)]
        arena_cols = max(sum(n for _, n in stage0), sum(n for _, n in later))
        A, D = [], []
        for k in range(2):
            arena = sb(f"arena{k}", arena_cols)
            for parts, table in [(A, stage0), (D, later)]:
                t, at = {}, 0
                for name, cols in table:
                    t[name] = arena[:, at:at + cols]
                    at += cols
                parts.append(t)
            for t, names in [(A[k], [("st", 12), ("ag", 8), ("gn", 4), ("m", 16), ("v", 16), ("r", 16)])]:
                for name, cols in names:
                    t[name] = sb(f"{name}{k}", cols)
                    D[k][name] = t[name]
            d = D[k]
            d["BCS"] = d["BCS"].bitcast(bf16)
            d["HI"] = d["HI"].bitcast(bf16)
            for name, w in [("N2", 0), ("XC", 1), ("SQ", 2), ("XN", 3), ("XI", 0), ("V1", 1), ("T1", 1),
                            ("A2", 2), ("T2", 3), ("X3", 4), ("OT", 5)]:
                d[name] = d[f"W{w}"]
        UU = [D[0]["W4"], D[0]["W5"], D[1]["W4"], D[1]["W5"]]
        DA, DB, HS = [[D[0][f"W{2 * m + q}"] for q in range(2)] for m in range(3)]
        CB, HC = [[D[1][f"W{2 * m + q}"] for q in range(2)] for m in range(2)]

        block = ctx.enter_context(nc.Block())

        def img(t):
            return t[:, 0:L].rearrange("p (h w) -> p h w", h=H)

        def frm(t):
            return t[:, 0:FRAME].rearrange("p (h w) -> p h w", h=H + 2)

        def wrapped(t):
            return t[:, :].rearrange("p (h w) -> p h w", h=H)

        def blk(t, k):
            return t[:, k * P:(k + 1) * P]

        def half(t, n):
            return t[:, n * BANK:(n + 1) * BANK]

        N2 = D_STATE // 2

        def two_images(j, name):
            return D[j // 2][name][:, (j % 2) * L:(j % 2) * L + L]

        def plain(eng):
            eng.sem_inc(S("waited"), 1)

        ONE = 1
        PRIMED = ["mix0", "mix1", "bcs0", "bcs1", "stored", "scan0", "scan1", "hc0", "hc1", "dbu0", "dbu1",
                  "cb0", "cb1", "sum0", "sum1", "y_read"]

        def sobel_sums(eng, tt, k, h):
            fr, sob = frm(A[k]["fr"]), S(f"a{k}_sob")
            eng.wait_ge(S(f"a{k}_fri"), 4 * h + 4)
            tt(A[k]["X"].rearrange("p (h w) -> p h w", w=W), fr[:, :, 0:32], fr[:, :, 2:34], ALU.add).then_inc(sob, 1)
            tt(A[k]["Y"].rearrange("p (h w) -> p h w", w=W), fr[:, :, 2:34], fr[:, :, 0:32], ALU.subtract).then_inc(sob, 1)

        x_pix = x.rearrange("b (k q) w c -> b (q w) k c", q=4)
        out_v = out.rearrange("b l (kb kq) c -> b kq l kb c", kq=4)

        @block.sync
        def _(sp):
            for name in PRIMED:
                sp.sem_inc(S(name), 1)
            sp.dma_start(vecs[:, :], vec).then_inc(S("vecs"), 16)
            sp.dma_start(mat[:, :], mats).then_inc(S("mats"), 16)
            for dst, src in [(convw, conv_w), (inw, in_w), (xbcw, xbc_w), (xdtw, xdt_w), (dtpw, dtp_w),
                             (outw, out_w), (projw, proj_w)]:
                sp.dma_start(dst[:, :], src).then_inc(S("weights"), 16)
            with sp.Fori(0, HALVES) as h:
                for k in range(2):
                    sp.wait_ge(S("ot"), 2 * h + k + 1)
                    plain(sp)
                    for kq in range(4):
                        src = D[k]["OT"][32 * kq:32 * kq + 32, :].rearrange("l (kb b c) -> l kb b c", b=2, c=C)
                        for b in range(2):
                            sp.dma_start(out_v[4 * h + 2 * k + b][kq], src[:, :, b]).then_inc(S("stored"), 16)
            sp.wait_ge(S("stored"), ONE + 256 * HALVES)

        @block.gpsimd
        def _(pool):
            tt = nc.gpsimd.tensor_tensor
            pool.memset(cpow[:, :], -0.5).then_inc(S("constants"), 1)
            pool.wait_ge(S("constants"), 1)
            pool.wait_ge(S("bn_var"), 3)
            tt(par[:, 6:9], par[:, 6:9], cpow[:, 0:3], ALU.pow).then_inc(S("bn_rstd"), 1)

            def root(t, wait, n, done):
                pool.wait_ge(S(wait), n)
                tt(t["gn"][:, 0:1], t["gn"][:, 0:1], cpow[:, 0:1], ALU.pow).then_inc(S(done), 1)

            def layer_root(t, n):
                pool.wait_ge(S("lvar"), n)
                tt(t["r"][:, :], t["v"][:, :], cpow[:, :], ALU.pow).then_inc(S("lrstd"), 1)

            with pool.Fori(0, HALVES) as h:
                for k in range(2):
                    for b in range(2):
                        dst = D[k]["R1"].rearrange("p (k b c) -> p b k c", b=2, c=C)[:, b]
                        pool.dma_start(dst, x_pix[4 * h + 2 * k + b]).then_inc(S(f"loaded{k}"), 16)
                for k in range(2):
                    root(A[k], "gvar", 8 * h + k + 1, "grstd")
                sobel_sums(pool, tt, 1, h)
                for k in range(2):
                    a = A[k]
                    pool.wait_ge(S("a_XYone"), 2 * h + k + 1)
                    tt(a["XY"][:, 0:L], a["X"][:, 0:L], a["Y"][:, 0:L], ALU.mult).then_inc(S("a_XY"), 1)
                for k in range(2):
                    a = A[k]
                    pool.wait_ge(S("a_D"), 2 * h + k + 1)
                    pool.wait_ge(S(f"a{k}_gg1"), 2 * h + 1)
                    tt(a["G1"][:, :], a["g1"][:, :], a["Dc"][:, :], ALU.mult).then_inc(S(f"a{k}_G"), 1)
                    pool.wait_ge(S(f"a{k}_gg1"), 2 * h + 2)
                    tt(a["G"][:, :], a["g"][:, :], a["Dc"][:, :], ALU.mult).then_inc(S(f"a{k}_G"), 1)
                    f_in = frm(a["fz"])[:, 1:33, 1:33]
                    pool.wait_ge(S("a_P0"), 2 * h + k + 1)
                    tt(img(a["Sc"]), img(a["Sc"]), f_in, ALU.mult).then_inc(S("a_Sc"), 1)
                    pool.wait_ge(S(f"a{k}_G"), 2 * h + 2)
                    pool.wait_ge(S("a_div"), 2 * h + k + 1)
                    tt(img(a["g"]), img(a["P0"]), f_in, ALU.mult).then_inc(S(f"a{k}_Wc"), 1)
                with pool.Fori(0, STEPS) as t:
                    for k in range(2):
                        a = A[k]
                        pool.wait_ge(S(f"a{k}_h"), (STEPS + 1) * h + t + 1)
                        pool.wait_ge(S(f"mix{k}"), ONE + STEPS * h + t)
                        pool.wait_ge(S("a_Pe"), 2 * h + k + 1)
                        pool.wait_ge(S("a_Sc"), 2 * h + k + 1)
                        hc = wrapped(a["hw"])[:, :, 1:33]
                        tt(img(a["X"]), img(a["Pe"]), hc, ALU.mult).then_inc(S(f"a{k}_e"), 1)
                        pool.wait_ge(S(f"a{k}_Wc"), (STEPS + 1) * h + t + 1)
                        tt(a["G1"][:, :], a["g"][:, :], a["Sc"][:, :], ALU.add).then_inc(S(f"a{k}_U"), 1)
                        pool.wait_ge(S(f"a{k}_U"), STEPS * h + t + 1)
                        tt(img(a["g"]), img(a["P0"]), hc, ALU.mult).then_inc(S(f"a{k}_Wc"), 1)
                for k in range(2):
                    root(D[k], "gvar", 8 * h + 2 + k + 1, "grstd")
                for k in range(2):
                    root(D[k], "gvar", 8 * h + 4 + k + 1, "grstd")
                    layer_root(D[k], 4 * h + k + 1)

                def relu_part(j):
                    pool.wait_ge(S("sp"), 4 * h + j + 1)
                    pool.wait_ge(S(f"rx{j // 2}"), 2 * h + j % 2 + 1)
                    du = two_images(j, "DU")
                    tt(du, du, two_images(j, "DL"), ALU.subtract).then_inc(S("spw"), 1)

                def delta_u(j):
                    pool.wait_ge(S("delta"), 4 * h + j + 1)
                    tt(two_images(j, "DU"), two_images(j, "DL"), two_images(j, "XS"), ALU.mult).then_inc(S("du"), 1)

                relu_part(0)
                relu_part(1)
                delta_u(0)
                relu_part(2)
                delta_u(1)
                for part in range(8):
                    with pool.Fori(N2 // 2 * part, N2 // 2 * (part + 1)) as n2:
                        for q in range(2):
                            done = 4 * N2 * h + n2
                            pool.wait_ge(S(f"scan{q}"), ONE + done + 1)
                            pool.wait_ge(S(f"cb{q}"), ONE + done + 1)
                            pool.wait_ge(S(f"sum{q}"), ONE + done)
                            tt(HC[q], HS[q], CB[q], ALU.mult).then_inc(S(f"hc{q}"), 1)
                    if part == 0:
                        relu_part(3)
                    if part in (1, 3):
                        delta_u(2 + part // 2)
                for k in range(2):
                    layer_root(D[k], 4 * h + 2 + k + 1)
                for k in range(2):
                    root(D[k], "gvar", 8 * h + 6 + k + 1, "grstd")

        @block.tensor
        def _(pe):
            mm = nc.tensor.matmul
            pe.wait_ge(S("mats"), 16)
            pe.wait_ge(S("weights"), 16 * 7)
            mm(PS[3][:, 0:P], xdtw[:, :], dtpw[:, :], start=True, stop=True).then_inc(S("dtw_ps"), 1)
            pe.wait_ge(S("dtw"), 1)
            pe.wait_ge(S("diag"), len(PE_TAPS) + 1)

            def transposes(src, dst):
                for n in range(BLK):
                    last = nc.tensor.transpose(blk(dst, n), blk(src, n), ident)
                return last

            def group_mean(t, k, n):
                pe.wait_ge(S("stats"), n)
                mm(PS[2 * k + 1][:, 0:2], mt("group_mean"), t["ag"][:, 0:2], start=True, stop=True).then_inc(S("gmean"), 1)

            def conv_taps(ps, taps, frame, n, chosen, first=0):
                for tap in chosen:
                    dy, dx = tap // 3, tap % 3
                    last = mm(half(ps, n), taps(tap), frame[:, dy + HB * n:dy + HB * n + HB, dx:dx + W],
                              start=(tap == first), stop=(tap == 8))
                return last

            def project(ps, w, src):
                for n in range(2):
                    last = mm(half(ps, n)[0:w.shape[1], :], w, half(src, n), start=True, stop=True)
                return last

            with pe.Fori(0, HALVES) as h:
                for k in range(2):
                    pe.wait_ge(S(f"loaded{k}"), 32 * h + 32)
                    transposes(D[k]["R1"], PS[2 * k]).then_inc(S("a_xT"), 1)
                for k in range(2):
                    group_mean(A[k], k, 8 * h + k + 1)

                def depthwise(k, w):
                    pe.wait_ge(S("a_fz"), 2 * h + k + 1)
                    pe.wait_ge(S("gvar"), 8 * h + k + 1)
                    for n in range(2):
                        last = conv_taps(PS[2 * k + 1 - w], lambda tap: blk(diag, 9 * (1 - w) + tap), frm(A[k]["fz"]),
                                         n, range(OFF_PE, 9), OFF_PE)
                    last.then_inc(S(f"a_conv{w}"), 1)

                def divergence(k):
                    a = A[k]
                    pe.wait_ge(S(f"a{k}_gg1"), 2 * h + 2)
                    g, ps = img(a["g"]), img(PS[2 * k])
                    for n in range(2):
                        r = slice(HB * n, HB * n + HB)
                        mm(ps[:, r, :], mt("roll_diff"), img(a["g1"])[:, r, :], start=True, stop=False)
                        mm(ps[:, r, 0:31], ident, g[:, r, 1:32], start=False, stop=False)
                        mm(ps[:, r, 31:32], ident, g[:, r, 0:1], start=False, stop=False)
                        mm(ps[:, r, 1:32], mt("neg_ident"), g[:, r, 0:31], start=False, stop=False)
                        last = mm(ps[:, r, 0:1], mt("neg_ident"), g[:, r, 31:32], start=False, stop=True)
                    last.then_inc(S("a_div"), 1)

                def rolls(k):
                    a = A[k]
                    pe.wait_ge(S("a_Py"), 4 * h + 2 * k + 1)
                    project(PS[2 * k + 1], mt("roll_down"), a["Pmy"]).then_inc(S("a_rollm"), 1)
                    pe.wait_ge(S("a_Py"), 4 * h + 2 * k + 2)
                    pe.wait_ge(S("a_Pe"), 2 * h + k + 1)
                    project(PS[2 * k], mt("roll_up"), a["R"]).then_inc(S("a_rollp"), 1)

                depthwise(0, 0)
                depthwise(0, 1)
                depthwise(1, 0)
                divergence(0)
                depthwise(1, 1)
                rolls(0)
                divergence(1)
                rolls(1)
                with pe.Fori(0, STEPS) as t:
                    for k in range(2):
                        a = A[k]
                        it = STEPS * h + t
                        for name, count, mname, src in [("c", 2 * it + 1, "roll_up", "Pmy"), ("c", 2 * it + 2, "roll_down", "sden"),
                                                        ("e", it + 1, "ident", "X"), ("ab", it + 1, "ident", "R")]:
                            pe.wait_ge(S(f"a{k}_{name}"), count)
                            if mname == "roll_up":
                                pe.wait_ge(S("a_Q6"), 2 * h + k + 1)
                                pe.wait_ge(S(f"a{k}_h"), (STEPS + 1) * h + t + 1)
                            for n in range(2):
                                last = mm(half(PS[2 * k], n), mt(mname), half(a[src], n), start=(mname == "roll_up"), stop=(name == "ab"))
                        last.then_inc(S(f"mix{k}"), 1)

                def conv_part(k, n, chosen):
                    return conv_taps(PS[2 * k], lambda tap: blk(convw, tap), frm(D[k]["cfz"]), n, chosen)

                def n2_pixels(k):
                    pe.wait_ge(S("n2"), 2 * h + k + 1)
                    transposes(D[k]["N2"], PS[2 * k]).then_inc(S("n2T"), 1)

                def xn_channels(k):
                    pe.wait_ge(S("xn"), 2 * h + k + 1)
                    transposes(D[k]["XN"], PS[2 * k + 1]).then_inc(S("xnT"), 1)

                group_mean(D[0], 0, 8 * h + 2 + 1)
                pe.wait_ge(S("c_fz"), 2 * h + 1)
                conv_part(0, 0, range(9))
                group_mean(D[1], 1, 8 * h + 2 + 2)
                conv_part(0, 1, range(9)).then_inc(S("c_conv"), 1)
                pe.wait_ge(S("c_fz"), 2 * h + 2)
                conv_part(1, 0, range(5))
                group_mean(D[0], 0, 8 * h + 4 + 1)
                conv_part(1, 0, range(5, 9))
                n2_pixels(0)
                conv_part(1, 1, range(9)).then_inc(S("c_conv"), 1)
                def in_proj(k, b):
                    d, i = D[k], 2 * h + b
                    pe.wait_ge(S("xnc"), 2 * h + k + 1)
                    if b == 1:
                        pe.wait_ge(S(f"rx{k}"), i)
                    for n in range(2):
                        last = mm(half(PS[2 * k], n), inw[:, 2 * P * b:2 * P * b + P], half(d["XNC"], n), start=True, stop=True)
                    last.then_inc(S(f"xi{k}"), 1)
                    if b == 1:
                        pe.wait_ge(S(f"r1{k}"), i)
                    for n in range(2):
                        last = mm(half(PS[2 * k + 1], n), inw[:, 2 * P * b + P:2 * P * b + 2 * P], half(d["XNC"], n), start=True, stop=True)
                    last.then_inc(S(f"z{k}"), 1)

                def x_proj(k, b):
                    i = 2 * h + b
                    xs = D[k]["XS"][:, b * L:b * L + L]
                    pe.wait_ge(S(f"xs{k}"), i + 1)
                    project(PS[2 * k], dtw[:, :], xs).then_inc(S(f"dt{k}"), 1)
                    pe.wait_ge(S(f"sz{k}"), i + 1)
                    project(PS[2 * k + 1], xbcw[:, :], xs).then_inc(S(f"bc{k}"), 1)

                xn_channels(0)
                group_mean(D[1], 1, 8 * h + 4 + 2)
                in_proj(0, 0)
                n2_pixels(1)
                x_proj(0, 0)
                in_proj(0, 1)
                xn_channels(1)
                in_proj(1, 0)
                x_proj(0, 1)
                x_proj(1, 0)
                in_proj(1, 1)

                def b_rows(j, n2, q):
                    pe.wait_ge(S(f"dbu{q}"), ONE + N2 * (4 * h + j) + n2)
                    for n in range(2):
                        last = mm(half(PS[q], n), sel[:, bass.ds((2 * n2 + q) * P, P)], half(two_images(j, "BCS"), n)[0:96, :], start=True, stop=True)
                    last.then_inc(S(f"bb{q}"), 1)

                def c_rows(j, n2, q):
                    pe.wait_ge(S(f"cb{1 - q}"), ONE + N2 * (4 * h + j) + n2 + q)
                    for n in range(2):
                        last = mm(half(PS[2], n), sel[:, bass.ds((2 * n2 + q + D_STATE) * P, P)], half(two_images(j, "BCS"), n)[0:96, :], start=True, stop=True)
                    last.then_inc(S(f"cps{q}"), 1)

                def rows_of(j, n2, q):
                    if j < 4:
                        b_rows(j, n2, q)
                        c_rows(j, n2, q)

                def sum_of(j, n2, q, start=False):
                    pe.wait_ge(S(f"hc{q}"), ONE + N2 * (4 * h + j) + n2 + 1)
                    for n in range(2):
                        last = mm(half(PS[3], n), ident, half(HC[q], n), start=start, stop=True, skip_group_check=True)
                    last.then_inc(S(f"sum{q}"), 1)

                def skip(k):
                    for n in range(BLK):
                        mm(blk(PS[2 * k], n), blk(D[k]["XNC"], n), skipI[:, :], start=(n % 4 == 0), stop=False, skip_group_check=True)

                def out_proj(j):
                    k, b = j // 2, j % 2
                    pe.wait_ge(S("y_read"), ONE + 4 * h + j + 1)
                    for n in range(BLK):
                        last = mm(blk(PS[2 * k], n)[:, C * b:C * b + C], blk(D[k]["SZ"], BLK * b + n), outw[:, :],
                                  start=False, stop=True, skip_group_check=True)
                    if b == 1:
                        last.then_inc(S("mo"), 1)

                pe.wait_ge(S("r10"), 2 * h + 2)
                pe.wait_ge(S("rx0"), 2 * h + 2)
                pe.wait_ge(S("bcs0"), ONE + 2 * h + 2)
                plain(pe)
                b_rows(0, 0, 0)
                b_rows(0, 0, 1)
                x_proj(1, 1)
                pe.wait_ge(S("rx1"), 2 * h + 2)
                plain(pe)
                c_rows(0, 0, 0)
                c_rows(0, 0, 1)
                rows_of(0, 1, 0)
                pe.wait_ge(S("r11"), 2 * h + 2)
                for j in range(4):
                    pe.wait_ge(S("y_read"), ONE + 4 * h + j)
                    plain(pe)
                    sum_of(j, 0, 0, start=True)
                    for n in range(2):
                        mm(half(PS[3], n), diagD[:, :], half(two_images(j, "XS"), n), start=False, stop=True, skip_group_check=True)
                    rows_of(j, 1, 1)
                    sum_of(j, 0, 1)
                    rows_of(j, 2, 0)
                    with pe.Fori(1, N2 - 2) as n2:
                        sum_of(j, n2, 0)
                        rows_of(j, n2 + 1, 1)
                        sum_of(j, n2, 1)
                        rows_of(j, n2 + 2, 0)
                    sum_of(j, N2 - 2, 0)
                    rows_of(j, N2 - 1, 1)
                    sum_of(j, N2 - 2, 1)
                    if j == 1:
                        pe.wait_ge(S("bcs1"), ONE + 2 * h + 2)
                        plain(pe)
                    if j == 3:
                        pe.wait_ge(S("dbu0"), ONE + N2 * (4 * h + 4))
                        skip(0)
                    rows_of(j + 1, 0, 0)
                    sum_of(j, N2 - 1, 0)
                    rows_of(j + 1, 0, 1)
                    sum_of(j, N2 - 1, 1)
                    rows_of(j + 1, 1, 0)
                out_proj(0)
                out_proj(1)
                pe.wait_ge(S("cb1"), ONE + N2 * (4 * h + 4))
                skip(1)
                out_proj(2)
                out_proj(3)
                for k in range(2):
                    pe.wait_ge(S("xn2"), 2 * h + k + 1)
                    transposes(D[k]["XN"], PS[2 * k + 1]).then_inc(S("xn2T"), 1)
                for k in range(2):
                    pe.wait_ge(S("v1"), 2 * h + k + 1)
                    project(PS[2 * k], projw[:, :], D[k]["V1"]).then_inc(S("proj"), 1)
                def x3_pixels(k):
                    pe.wait_ge(S("X3"), 2 * h + k + 1)
                    transposes(D[k]["X3"], PS[2 * k]).then_inc(S("n3T"), 1)

                def first_dct(k):
                    pe.wait_ge(S("t1"), 2 * h + k + 1)
                    pe.wait_ge(S("gvar"), 8 * h + 6 + k + 1)
                    for n in range(BLK):
                        last = mm(blk(PS[2 * k + 1], n), blk(D[k]["T1"], n), mt("dct"), start=True, stop=True, skip_group_check=True)
                    last.then_inc(S("dct1"), 1)

                def a2_pixels(k):
                    pe.wait_ge(S("a2"), 2 * h + k + 1)
                    transposes(D[k]["A2"], PS[2 * k]).then_inc(S("a2T"), 1)
                    for n in range(BLK):
                        mm(blk(PS[2 * k + 1], n), blk(D[k]["X3"], n), ident, start=(n % 4 == 0), stop=False, skip_group_check=True)

                def second_dct(k):
                    pe.wait_ge(S("t2"), 2 * h + k + 1)
                    for n in range(2):
                        last = mm(half(PS[2 * k + 1], n), mt("dct"), half(D[k]["T2"], n), start=False, stop=True, skip_group_check=True)
                    last.then_inc(S("final"), 1)

                x3_pixels(0)
                group_mean(D[0], 0, 8 * h + 6 + 1)
                first_dct(0)
                x3_pixels(1)
                group_mean(D[1], 1, 8 * h + 6 + 2)
                a2_pixels(0)
                first_dct(1)
                second_dct(0)
                a2_pixels(1)
                second_dct(1)

        @block.scalar
        def _(act):
            def av(out_, in_, func, scale=1.0, bias=0.0):
                return nc.scalar.activation(out_, in_, func, bias=bias, scale=scale)

            def gnorm(t, out_, in_, n):
                act.wait_ge(S("gshift"), n)
                return av(out_, in_, ACT.Identity, t["gn"][:, 0:1], t["gn"][:, 1:2])

            act.wait_ge(S("dtw_ps"), 1)
            av(dtw[:, :], PS[3][:, 0:P], ACT.Identity).then_inc(S("dtw"), 1)
            act.wait_ge(S("vecs"), 16)
            av(Amat[:, :], vecs[:, V_ALOG:V_ALOG + D_STATE], ACT.Exp).then_inc(S("Aexp"), 1)
            act.wait_ge(S("par"), 6)
            act.wait_ge(S("frames"), 2)
            with act.Fori(0, HALVES) as h:
                for k in range(2):
                    act.wait_ge(S("a_xT"), 2 * h + k + 1)
                    av(xres[k][:, :], PS[2 * k][:, :], ACT.Identity).then_inc(S("a_x"), 1)
                for k in range(2):
                    a = A[k]
                    act.wait_ge(S("a_x"), 2 * h + k + 1)
                    gnorm(a, frm(a["fz"])[:, 1:33, 1:33], img(xres[k]), 8 * h + k + 1).then_inc(S("a_fz"), 1)

                def frames(k):
                    a = A[k]
                    fr = frm(a["fr"])
                    gnorm(a, fr[:, 1:33, 1:33], img(xres[k]), 8 * h + k + 1).then_inc(S(f"a{k}_fri"), 1)
                    act.wait_ge(S(f"a{k}_fri"), 4 * h + 1)
                    av(fr[:, 1:33, 0:1], fr[:, 1:33, 2:3], ACT.Identity).then_inc(S(f"a{k}_fri"), 1)
                    av(fr[:, 1:33, 33:34], fr[:, 1:33, 31:32], ACT.Identity).then_inc(S(f"a{k}_fri"), 1)
                    act.wait_ge(S(f"a{k}_fri"), 4 * h + 3)
                    av(fr[:, 0:1, :], fr[:, 2:3, :], ACT.Identity)
                    av(fr[:, 33:34, :], fr[:, 31:32, :], ACT.Identity).then_inc(S(f"a{k}_fri"), 1)
                    gnorm(a, wrapped(a["hw"])[:, :, 1:33], img(xres[k]), 8 * h + k + 1).then_inc(S(f"a{k}_h"), 1)

                def first_taps(k):
                    act.wait_ge(S("a_fz"), 2 * h + k + 1)
                    for name, w in [("g1", 0), ("g", 1)]:
                        col = V_WG + 9 * (1 - w)
                        av(img(A[k][name]), frm(A[k]["fz"])[:, 0:H, 0:W], ACT.Identity, vecs[:, col:col + 1]).then_inc(S("a_tap0"), 1)

                def squares(k):
                    a = A[k]
                    act.wait_ge(S("a_sobel"), 2 * h + k + 1)
                    av(a["Dc"][:, 0:L], a["R"][:, 0:L], ACT.Square, 0.5).then_inc(S(f"a{k}_sq"), 1)
                    av(a["Kx"][:, 0:L], a["XY"][:, 0:L], ACT.Square, 0.5).then_inc(S(f"a{k}_sq"), 1)
                    act.wait_ge(S(f"a{k}_sq"), 2 * h + 2)
                    av(a["X"][:, 0:L], a["Dc"][:, 0:L], ACT.Identity, 1.0, 1.0)
                    av(a["Y"][:, 0:L], a["Kx"][:, 0:L], ACT.Identity, 1.0, 1.0).then_inc(S("a_XYone"), 1)

                def reciprocal(k):
                    a = A[k]
                    act.wait_ge(S("a_den"), 4 * h + 2 * k + 2)
                    av(a["R"], a["sden"], ACT.Ln).then_inc(S("a_rec"), 1)
                    act.wait_ge(S("a_rec"), 4 * h + 2 * k + 1)
                    av(a["R"], a["R"], ACT.Exp, -1.0).then_inc(S("a_rec"), 1)

                def relu(k, w):
                    t = A[k]["g1" if w == 0 else "g"]
                    c = 2 - 2 * w
                    act.wait_ge(S("a_merge"), 4 * h + 2 * k + w + 1)
                    av(t, t, ACT.Relu, par[:, c:c + 1], par[:, c + 1:c + 2]).then_inc(S(f"a{k}_gg1"), 1)

                def from_D(k):
                    a = A[k]
                    act.wait_ge(S("a_D"), 2 * h + k + 1)
                    act.wait_ge(S("stored"), ONE + 256 * h)
                    plain(act)
                    av(a["P0"], a["Dc"], ACT.Identity, 2.0, -1.0)
                    av(a["Sc"], a["Dc"], ACT.Identity, 2 * DT).then_inc(S("a_P0"), 1)

                def wrap(k, t):
                    hw = wrapped(A[k]["hw"])
                    act.wait_ge(S(f"a{k}_h"), (STEPS + 1) * h + t + 1)
                    av(hw[:, :, 0:1], hw[:, :, 32:33], ACT.Identity)
                    av(hw[:, :, 33:34], hw[:, :, 1:2], ACT.Identity).then_inc(S(f"a{k}_wrap"), 1)

                frames(0)
                first_taps(0)
                frames(1)
                first_taps(1)
                squares(0)
                squares(1)
                reciprocal(0)
                relu(0, 0)
                relu(0, 1)
                reciprocal(1)
                from_D(0)
                relu(1, 0)
                from_D(1)
                relu(1, 1)
                for k in range(2):
                    wrap(k, 0)
                for k in range(2):
                    a = A[k]
                    act.wait_ge(S("a_rollm"), 2 * h + k + 1)
                    act.wait_ge(S("a_Pm"), 2 * h + k + 1)
                    av(a["Kx"][:, :], PS[2 * k + 1][:, :], ACT.Identity).then_inc(S("a_Q5"), 1)
                    act.wait_ge(S("a_rollp"), 2 * h + k + 1)
                    av(a["Ky"][:, :], PS[2 * k][:, :], ACT.Identity).then_inc(S("a_Q6"), 1)
                with act.Fori(1, STEPS) as t:
                    for k in range(2):
                        wrap(k, t)
                for k in range(2):
                    a = A[k]
                    act.wait_ge(S(f"a{k}_h"), (STEPS + 1) * h + STEPS + 1)
                    av(img(a["X"]), wrapped(a["hw"])[:, :, 1:33], ACT.Relu, par[:, 4:5], par[:, 5:6]).then_inc(S("a_bnout"), 1)
                    gnorm(D[k], frm(D[k]["cfz"])[:, 1:33, 1:33], img(xres[k]), 8 * h + 2 + k + 1).then_inc(S("c_fz"), 1)

                def norm2(k):
                    gnorm(D[k], D[k]["N2"], D[k]["X2"], 8 * h + 4 + k + 1).then_inc(S("n2"), 1)

                def square(k, g):
                    act.wait_ge(S("xc"), 4 * h + 2 * g + k + 1)
                    av(D[k]["SQ"], D[k]["XC"], ACT.Square).then_inc(S("csq"), 1)

                def layer_scale(k):
                    act.wait_ge(S("xnT"), 2 * h + k + 1)
                    av(D[k]["XNC"], PS[2 * k + 1][:, :], ACT.Identity, vc("ln_g"), vc("ln_b")).then_inc(S("xnc"), 1)

                def silu_x(k, b):
                    i = 2 * h + b
                    act.wait_ge(S(f"cconv{k}"), 4 * i + 4)
                    av(D[k]["XS"][:, b * L:b * L + L], D[k]["XI"], ACT.Silu, 1.0, vc("m_conv_b")).then_inc(S(f"xs{k}"), 1)

                def first_part(k, b):
                    d, i = D[k], 2 * h + b
                    act.wait_ge(S(f"bc{k}"), i + 1)
                    if b == 1:
                        act.wait_ge(S(f"bcs{k}"), ONE + i)
                    av(d["HI"][0:96, :], PS[2 * k + 1][0:96, :], ACT.Identity).then_inc(S(f"bfpart{k}"), 1)

                def abs_x(k, b):
                    d, i, cols = D[k], 2 * h + b, slice(b * L, b * L + L)
                    act.wait_ge(S(f"dt{k}"), i + 1)
                    av(d["DL"][:, cols], PS[2 * k][:, :], ACT.Abs, 1.0, vc("m_dt_b")).then_inc(S(f"absx{k}"), 1)

                def exp_of(j):
                    act.wait_ge(S(f"absx{j // 2}"), 2 * h + j % 2 + 1)
                    av(two_images(j, "DL"), two_images(j, "DL"), ACT.Exp, -1.0).then_inc(S("ex"), 1)

                def ln_of(j):
                    act.wait_ge(S("sp"), 4 * h + j + 1)
                    av(UU[j], UU[j], ACT.Ln).then_inc(S("ln"), 1)

                def middle(k, b):
                    d, i, cols = D[k], 2 * h + b, slice(b * L, b * L + L)
                    act.wait_ge(S(f"r1{k}"), i + 1)
                    av(d["BCS"][0:96, cols], d["R1"][0:96, :], ACT.Identity).then_inc(S(f"bfpart{k}"), 1)

                def silu_z(k, b):
                    act.wait_ge(S(f"z{k}"), 2 * h + b + 1)
                    av(D[k]["SZ"][:, b * L:b * L + L], PS[2 * k + 1][:, :], ACT.Silu).then_inc(S(f"sz{k}"), 1)

                def decay(j, n2, q):
                    if j < 4:
                        act.wait_ge(S("delta"), 4 * h + j + 1)
                        act.wait_ge(S(f"scan{q}"), ONE + N2 * (4 * h + j) + n2)
                        plain(act)
                        av(DA[q], two_images(j, "DL"), ACT.Exp, Amat[:, bass.ds(2 * n2 + q, 1)]).then_inc(S(f"da{q}"), 1)

                def copy_c(j, n2, q):
                    act.wait_ge(S(f"cps{q}"), N2 * (4 * h + j) + n2 + 1)
                    act.wait_ge(S(f"hc{q}"), ONE + N2 * (4 * h + j) + n2)
                    av(CB[q], PS[2][:, :], ACT.Identity).then_inc(S(f"cb{q}"), 1)

                norm2(0)
                square(0, 0)
                layer_scale(0)
                norm2(1)
                silu_z(0, 0)
                silu_x(0, 0)
                square(1, 0)
                abs_x(0, 0)
                first_part(0, 0)
                middle(0, 0)
                layer_scale(1)
                silu_z(0, 1)
                silu_x(0, 1)
                silu_z(1, 0)
                abs_x(0, 1)
                silu_x(1, 0)
                first_part(0, 1)
                abs_x(1, 0)
                middle(0, 1)
                first_part(1, 0)
                middle(1, 0)
                for j in range(3):
                    exp_of(j)
                silu_z(1, 1)
                silu_x(1, 1)
                for j in range(3):
                    ln_of(j)
                abs_x(1, 1)
                decay(0, 0, 0)
                first_part(1, 1)
                copy_c(0, 0, 0)
                decay(0, 0, 1)
                copy_c(0, 0, 1)
                middle(1, 1)
                decay(0, 1, 0)
                exp_of(3)
                decay(0, 1, 1)
                for j in range(4):
                    with act.Fori(1 if j == 0 else 0, N2 - 1) as n2:
                        for q in range(2):
                            copy_c(j, n2, q)
                            decay(j, n2 + 1, q)
                    if j == 0:
                        ln_of(3)
                    for q in range(2):
                        copy_c(j, N2 - 1, q)
                        decay(j + 1, 0, q)
                square(0, 1)
                square(1, 1)
                for k in range(2):
                    act.wait_ge(S("xn2T"), 2 * h + k + 1)
                    av(D[k]["V1"], PS[2 * k + 1][:, :], ACT.Identity, vc("ln_g"), vc("ln_b")).then_inc(S("v1"), 1)
                def copy_x3(k):
                    act.wait_ge(S("n3T"), 2 * h + k + 1)
                    av(D[k]["T1"], PS[2 * k][:, :], ACT.Identity).then_inc(S("t1"), 1)

                def scale(k):
                    act.wait_ge(S("dct1"), 2 * h + k + 1)
                    act.wait_ge(S("gshift"), 8 * h + 6 + k + 1)
                    a2, ps = D[k]["A2"].rearrange("p (k w) -> p w k", k=H), PS[2 * k + 1][:, :].rearrange("p (w k) -> p w k", w=W)
                    av(a2[:, :, 1:H], ps[:, :, 1:H], ACT.Identity, D[k]["gn"][:, 0:1])
                    av(a2[:, :, 0:1], ps[:, :, 0:1], ACT.Identity, D[k]["gn"][:, 0:1], D[k]["gn"][:, 1:2]).then_inc(S("a2"), 1)

                def copy_a2(k):
                    act.wait_ge(S("a2T"), 2 * h + k + 1)
                    av(D[k]["T2"], PS[2 * k][:, :], ACT.Identity).then_inc(S("t2"), 1)

                def copy_out(k):
                    act.wait_ge(S("final"), 2 * h + k + 1)
                    av(D[k]["OT"], PS[2 * k + 1][:, :], ACT.Identity).then_inc(S("ot"), 1)

                copy_x3(0)
                scale(0)
                copy_x3(1)
                copy_a2(0)
                scale(1)
                copy_out(0)
                copy_a2(1)
                copy_out(1)

        @block.vector
        def _(dve):
            tt = nc.vector.tensor_tensor
            stt = nc.vector.scalar_tensor_tensor
            ts = nc.vector.tensor_scalar
            chain = [0]

            def link(ins):
                chain[0] += 1
                ins.then_inc(S("setup_step"), 1)
                dve.wait_ge(S("setup_step"), chain[0])

            dve.wait_ge(S("vecs"), 16)
            for n, name in enumerate(["g", "g1", "out"]):
                ts(par[:, 6 + n:7 + n], vc(name + "_var"), BN_EPS, None, ALU.add).then_inc(S("bn_var"), 1)
            dve.wait_ge(S("mats"), 16)
            for t in PE_TAPS:
                ts(blk(diag, t), ident, vecs[:, V_WG + t:V_WG + t + 1], None, ALU.mult).then_inc(S("diag"), 1)
            ts(skipI[:, :], ident, vc("skip"), None, ALU.mult)
            ts(diagD[:, :], ident, vc("m_D"), None, ALU.mult)
            nc.vector.tensor_copy(sel[:, :].rearrange("k (j m) -> k j m", m=P),
                                  vecs[0:96, NVEC:NVEC + 32].unsqueeze(2).to_broadcast([96, 32, P])).then_inc(S("diag"), 1)
            for k in range(2):
                dve.memset(A[k]["fz"], 0.0).then_inc(S("frames"), 1)
            dve.wait_ge(S("Aexp"), 1)
            link(ts(Amat[:, :], Amat[:, :], -1.0, None, ALU.mult))
            dve.wait_ge(S("bn_rstd"), 1)
            for n, (name, f) in enumerate([("g", DT), ("g1", DT), ("out", 1.0)]):
                link(stt(par[:, 9:10], vc(name + "_gamma"), f, par[:, 6 + n:7 + n], ALU.mult, ALU.mult))
                link(tt(par[:, 10:11], vc(name + "_mean"), par[:, 9:10], ALU.mult))
                ts(par[:, 2 * n:2 * n + 1], par[:, 9:10], 1.0, None, ALU.mult).then_inc(S("par"), 1)
                stt(par[:, 2 * n + 1:2 * n + 2], vc(name + "_beta"), f, par[:, 10:11], ALU.mult, ALU.subtract).then_inc(S("par"), 1)
                dve.wait_ge(S("par"), 2 * n + 2)

            def stats(src, t, h, g, k):
                step, n0 = S(f"gstep{k}"), 20 * h + 5 * g
                nc.vector.bn_stats(t["st"][:, 0:6], half(src, 0)).then_inc(step, 1)
                nc.vector.bn_stats(t["st"][:, 6:12], half(src, 1)).then_inc(step, 1)
                dve.wait_ge(step, n0 + 2)
                plain(dve)
                nc.vector.bn_aggr(t["ag"][:, 0:2], t["st"][:, :]).then_inc(step, 1)
                dve.wait_ge(step, n0 + 3)
                stt(t["ag"][:, 1:2], t["ag"][:, 0:1], t["ag"][:, 0:1], t["ag"][:, 1:2], ALU.mult, ALU.add).then_inc(S("stats"), 1)

            def group_var(t, h, g, k):
                step, n0, n = S(f"gstep{k}"), 20 * h + 5 * g + 3, 8 * h + 2 * g + k + 1
                dve.wait_ge(S("gmean"), n)
                ts(t["ag"][:, 2:4], PS[2 * k + 1][:, 0:2], 1.0, None, ALU.mult).then_inc(step, 1)
                dve.wait_ge(step, n0 + 1)
                stt(t["ag"][:, 4:5], t["ag"][:, 2:3], t["ag"][:, 2:3], t["ag"][:, 3:4], ALU.mult, ALU.subtract).then_inc(step, 1)
                dve.wait_ge(step, n0 + 2)
                ts(t["gn"][:, 0:1], t["ag"][:, 4:5], -1.0, GN_EPS, ALU.mult, ALU.add).then_inc(S("gvar"), 1)

            def group_shift(t, h, g, k):
                dve.wait_ge(S("grstd"), 8 * h + 2 * g + k + 1)
                stt(t["gn"][:, 1:2], t["ag"][:, 2:3], -(H ** 0.5) if g == 3 else -1.0, t["gn"][:, 0:1], ALU.mult, ALU.mult).then_inc(S("gshift"), 1)

            def group_norms(ts_, h, g):
                for k in range(2):
                    group_var(ts_[k], h, g, k)
                for k in range(2):
                    group_shift(ts_[k], h, g, k)

            def group_norm(t, h, g, k):
                group_var(t, h, g, k)
                group_shift(t, h, g, k)

            def v3(t):
                return t[:, :].rearrange("p (g c) -> p g c", c=C)

            def center(k, h, g):
                d, step, n0 = D[k], S(f"lstep{k}"), 6 * h + 3 * g
                dve.wait_ge(S(["n2T", "mo"][g]), 2 * h + k + 1)
                nc.vector.reduce_sum(d["m"][:, :], v3(PS[2 * k]), axis=AX.X).then_inc(step, 1)
                dve.wait_ge(step, n0 + 1)
                ts(d["m"][:, :], d["m"][:, :], 1.0 / C, None, ALU.mult).then_inc(step, 1)
                dve.wait_ge(step, n0 + 2)
                tt(v3(d["XC"]), v3(PS[2 * k]), d["m"][:, :].unsqueeze(2).to_broadcast([P, 16, C]), ALU.subtract).then_inc(S("xc"), 1)

            def variance(k, h, g):
                d, step, n0 = D[k], S(f"lstep{k}"), 6 * h + 3 * g
                dve.wait_ge(S("csq"), 4 * h + 2 * g + k + 1)
                nc.vector.reduce_sum(d["v"][:, :], v3(d["SQ"]), axis=AX.X).then_inc(step, 1)
                dve.wait_ge(step, n0 + 3)
                ts(d["v"][:, :], d["v"][:, :], 1.0 / C, LN_EPS, ALU.mult, ALU.add).then_inc(S("lvar"), 1)

            def normalize(k, h, g):
                d = D[k]
                dve.wait_ge(S("lrstd"), 4 * h + 2 * g + k + 1)
                tt(v3(d["XN"]), v3(d["XC"]), d["r"][:, :].unsqueeze(2).to_broadcast([P, 16, C]), ALU.mult).then_inc(S(["xn", "xn2"][g]), 1)

            with dve.Fori(0, HALVES) as h:
                for k in range(2):
                    dve.wait_ge(S("a_x"), 2 * h + k + 1)
                    stats(xres[k], A[k], h, 0, k)
                group_norms(A, h, 0)

                def sobel(k):
                    a = A[k]
                    fr = frm(a["fr"])
                    X = a["X"].rearrange("p (h w) -> p h w", w=W)
                    Y = a["Y"].rearrange("p (h w) -> p h w", w=W)
                    sob = S(f"a{k}_sob")
                    if k == 0:
                        sobel_sums(dve, tt, 0, h)
                    dve.wait_ge(sob, 4 * h + 1)
                    stt(X, fr[:, :, 1:33], 2.0, X, ALU.mult, ALU.add).then_inc(sob, 1)
                    dve.wait_ge(sob, 4 * h + 3)
                    tt(img(a["XY"]), Y[:, 0:32, :], Y[:, 2:34, :], ALU.add).then_inc(sob, 1)
                    tt(img(a["R"]), X[:, 2:34, :], X[:, 0:32, :], ALU.subtract)
                    dve.wait_ge(sob, 4 * h + 4)
                    stt(img(a["XY"]), Y[:, 1:33, :], 2.0, img(a["XY"]), ALU.mult, ALU.add).then_inc(S("a_sobel"), 1)

                def taps(k, w):
                    t = img(A[k]["g1" if w == 0 else "g"])
                    i = 4 * h + 2 * k + w
                    dve.wait_ge(S("a_tap0"), i + 1)
                    for tap in range(1, OFF_PE):
                        if tap > 1:
                            dve.wait_ge(S("a_tap"), (OFF_PE - 1) * i + tap - 1)
                        col = V_WG + 9 * (1 - w) + tap
                        stt(t, frm(A[k]["fz"])[:, 0:H, tap:tap + W], vecs[:, col:col + 1], t, ALU.mult, ALU.add).then_inc(S("a_tap"), 1)

                def merge(k, w):
                    t = A[k]["g1" if w == 0 else "g"]
                    i = 4 * h + 2 * k + w
                    dve.wait_ge(S("a_tap"), (OFF_PE - 1) * (i + 1))
                    dve.wait_ge(S(f"a_conv{w}"), 2 * h + k + 1)
                    tt(t, t, PS[2 * k + 1 - w][:, :], ALU.add).then_inc(S("a_merge"), 1)

                def denominator(k):
                    a = A[k]
                    dve.wait_ge(S("a_XYone"), 2 * h + k + 1)
                    tt(a["sden"], a["X"][:, 0:L], a["Y"][:, 0:L], ALU.add).then_inc(S("a_den"), 1)
                    dve.wait_ge(S("a_XY"), 2 * h + k + 1)
                    dve.wait_ge(S("a_den"), 4 * h + 2 * k + 1)
                    stt(a["sden"], a["sden"], 2 * DT, a["XY"], ALU.mult, ALU.add).then_inc(S("a_den"), 1)

                def fractions(k):
                    a, newton = A[k], S("a_newton")
                    dve.wait_ge(S("a_rec"), 4 * h + 2 * k + 2)
                    tt(a["sden"], a["sden"], a["R"], ALU.mult).then_inc(newton, 1)
                    dve.wait_ge(newton, 4 * h + 2 * k + 1)
                    stt(a["R"], a["sden"], -2.0, a["R"], ALU.add, ALU.mult).then_inc(newton, 1)
                    dve.wait_ge(newton, 4 * h + 2 * k + 2)
                    stt(a["Dc"], a["XY"], -1.0, a["R"], ALU.mult, ALU.mult).then_inc(S("a_D"), 1)
                    stt(a["Kx"], a["Y"][:, 0:L], -2 * DT, a["R"], ALU.mult, ALU.mult)
                    stt(a["Ky"], a["X"][:, 0:L], -2 * DT, a["R"], ALU.mult, ALU.mult).then_inc(S("a_K"), 1)

                def y_neighbours(k):
                    a = A[k]
                    dve.wait_ge(S("a_K"), 2 * h + k + 1)
                    dve.wait_ge(S(f"a{k}_G"), 2 * h + 1)
                    tt(a["Pmy"], a["Ky"], a["G1"], ALU.subtract).then_inc(S("a_Py"), 1)
                    tt(a["R"], a["Ky"], a["G1"], ALU.add).then_inc(S("a_Py"), 1)

                def x_neighbours(k):
                    a = A[k]
                    dve.wait_ge(S(f"a{k}_G"), 2 * h + 2)
                    tt(a["Pmx"], a["Kx"], a["G"], ALU.subtract)
                    tt(a["G"], a["Kx"], a["G"], ALU.add).then_inc(S("a_Pm"), 1)

                def minus_E(k):
                    a = A[k]
                    dve.wait_ge(S("a_div"), 2 * h + k + 1)
                    tt(a["Pe"], a["Dc"], PS[2 * k][:, :], ALU.mult).then_inc(S("a_Pe"), 1)

                sobel(0)
                sobel(1)
                taps(0, 0)
                denominator(0)
                taps(0, 1)
                merge(0, 0)
                denominator(1)
                merge(0, 1)
                fractions(0)
                taps(1, 0)
                taps(1, 1)
                fractions(1)
                dve.wait_ge(S("stored"), ONE + 256 * h)
                plain(dve)

                def products(k, t, between=None):
                    a, it = A[k], STEPS * h + t
                    hw = wrapped(a["hw"])
                    hc = hw[:, :, 1:33]
                    dve.wait_ge(S("a_Q6"), 2 * h + k + 1)
                    dve.wait_ge(S(f"mix{k}"), ONE + it)
                    dve.wait_ge(S(f"a{k}_h"), (STEPS + 1) * h + t + 1)
                    tt(img(a["Pmy"]), img(a["Kx"]), hc, ALU.mult).then_inc(S(f"a{k}_c"), 1)
                    tt(img(a["sden"]), img(a["Ky"]), hc, ALU.mult).then_inc(S(f"a{k}_c"), 1)
                    if between:
                        between()
                    dve.wait_ge(S(f"a{k}_wrap"), it + 1)
                    tt(img(a["R"]), img(a["Pmx"]), hw[:, :, 0:32], ALU.mult)
                    tt(img(a["XY"]), img(a["G"]), hw[:, :, 2:34], ALU.mult).then_inc(S(f"a{k}_abm"), 1)
                    dve.wait_ge(S(f"a{k}_abm"), it + 1)
                    tt(a["R"], a["R"], a["XY"], ALU.add).then_inc(S(f"a{k}_ab"), 1)

                def new_h(k, t):
                    a = A[k]
                    dve.wait_ge(S(f"mix{k}"), ONE + STEPS * h + t + 1)
                    dve.wait_ge(S(f"a{k}_U"), STEPS * h + t + 1)
                    dve.wait_ge(S(f"a{k}_Wc"), (STEPS + 1) * h + t + 2)
                    tt(wrapped(a["hw"])[:, :, 1:33], img(PS[2 * k]), img(a["G1"]), ALU.add).then_inc(S(f"a{k}_h"), 1)

                y_neighbours(0)
                merge(1, 0)
                x_neighbours(0)
                merge(1, 1)
                minus_E(0)
                y_neighbours(1)
                products(0, 0)
                x_neighbours(1)
                minus_E(1)
                with dve.Fori(0, STEPS - 1) as t:
                    products(1, t)
                    new_h(0, t)
                    products(0, t + 1)
                    new_h(1, t)
                products(1, STEPS - 1, lambda: new_h(0, STEPS - 1))

                def add_stage0(k):
                    dve.wait_ge(S("a_bnout"), 2 * h + k + 1)
                    tt(xres[k][:, :], xres[k][:, :], A[k]["X"][:, 0:L], ALU.add).then_inc(S("x1"), 1)
                    dve.wait_ge(S("x1"), 2 * h + k + 1)
                    stats(xres[k], D[k], h, 1, k)

                def add_conv(k):
                    dve.wait_ge(S("c_conv"), 2 * h + k + 1)
                    stt(D[k]["X2"], PS[2 * k][:, :], vc("conv_bias"), xres[k][:, :], ALU.add, ALU.add).then_inc(S("X2"), 1)

                def x2_norm(k):
                    dve.wait_ge(S("X2"), 2 * h + k + 1)
                    stats(D[k]["X2"], D[k], h, 2, k)
                    group_norm(D[k], h, 2, k)

                add_stage0(0)
                new_h(1, STEPS - 1)
                group_norm(D[0], h, 1, 0)
                add_stage0(1)
                group_norm(D[1], h, 1, 1)
                add_conv(0)
                x2_norm(0)
                center(0, h, 0)
                variance(0, h, 0)
                add_conv(1)
                normalize(0, h, 0)
                x2_norm(1)

                def causal(k, b):
                    d, i = D[k], 2 * h + b
                    dve.wait_ge(S(f"xi{k}"), i + 1)
                    if b == 1:
                        dve.wait_ge(S(f"xs{k}"), i)
                    w = [vecs[:, V_CONVW + t:V_CONVW + t + 1] for t in range(4)]
                    ts(d["XI"], PS[2 * k][:, :], w[3], None, ALU.mult).then_inc(S(f"cconv{k}"), 1)
                    for t in range(1, 4):
                        dve.wait_ge(S(f"cconv{k}"), 4 * i + t)
                        stt(d["XI"][:, t:L], PS[2 * k][:, 0:L - t], w[3 - t], d["XI"][:, t:L], ALU.mult, ALU.add)\
                            .then_inc(S(f"cconv{k}"), 1)

                def rest(k, b):
                    d, i = D[k], 2 * h + b
                    dve.wait_ge(S(f"bfpart{k}"), 2 * i + 1)
                    tt(d["R1"][0:96, :], PS[2 * k + 1][0:96, :], d["HI"][0:96, :], ALU.subtract).then_inc(S(f"r1{k}"), 1)

                def parts(k, b):
                    d, i, cols = D[k], 2 * h + b, slice(b * L, b * L + L)
                    dve.wait_ge(S(f"bfpart{k}"), 2 * i + 2)
                    tt(d["BCS"][64:96, cols], d["R1"][64:96, :], d["BCS"][64:96, cols], ALU.subtract)
                    nc.vector.tensor_copy(d["BCS"][0:32, cols], d["HI"][0:32, :]).then_inc(S(f"bcs{k}"), 1)

                def relu_x(k, b):
                    dve.wait_ge(S(f"absx{k}"), 2 * h + b + 1)
                    ts(D[k]["DU"][:, b * L:b * L + L], PS[2 * k][:, :], vc("m_dt_b"), 0.0, ALU.add, ALU.max).then_inc(S(f"rx{k}"), 1)

                def one_plus(j):
                    e = two_images(j, "DL")
                    dve.wait_ge(S("ex"), 4 * h + j + 1)
                    ts(UU[j], e, 1.0, None, ALU.add).then_inc(S("uu"), 1)
                    dve.wait_ge(S("uu"), 4 * h + j + 1)
                    stt(e, UU[j], -1.0, e, ALU.add, ALU.subtract).then_inc(S("sp"), 1)

                def delta(j):
                    dve.wait_ge(S("ln"), 4 * h + j + 1)
                    dve.wait_ge(S("spw"), 4 * h + j + 1)
                    tt(two_images(j, "DL"), UU[j], two_images(j, "DU"), ALU.add).then_inc(S("delta"), 1)

                def scan_step(j, n2, q):
                    done = N2 * (4 * h + j) + n2
                    dve.wait_ge(S(f"bb{q}"), done + 1)
                    dve.wait_ge(S(f"scan{q}"), ONE + done)
                    tt(DB[q], two_images(j, "DU"), PS[q][:, :], ALU.mult).then_inc(S(f"dbu{q}"), 1)
                    dve.wait_ge(S(f"da{q}"), done + 1)
                    dve.wait_ge(S(f"dbu{q}"), ONE + done + 1)
                    dve.wait_ge(S(f"hc{q}"), ONE + done)
                    nc.vector.tensor_tensor_scan(HS[q], DA[q], DB[q], 0.0, ALU.mult, ALU.add).then_inc(S(f"scan{q}"), 1)

                causal(0, 0)
                center(1, h, 0)
                variance(1, h, 0)
                relu_x(0, 0)
                rest(0, 0)
                normalize(1, h, 0)
                parts(0, 0)
                causal(0, 1)
                causal(1, 0)
                relu_x(0, 1)
                rest(0, 1)
                relu_x(1, 0)
                parts(0, 1)
                rest(1, 0)
                causal(1, 1)
                one_plus(0)
                one_plus(1)
                parts(1, 0)
                one_plus(2)
                delta(0)
                delta(1)
                relu_x(1, 1)
                dve.wait_ge(S("du"), 4 * h + 1)
                scan_step(0, 0, 0)
                rest(1, 1)
                scan_step(0, 0, 1)
                parts(1, 1)
                delta(2)
                one_plus(3)
                def gate(j):
                    dve.wait_ge(S("sum1"), ONE + N2 * (4 * h + j + 1))
                    tt(two_images(j, "SZ"), PS[3][:, :], two_images(j, "SZ"), ALU.mult).then_inc(S("y_read"), 1)

                for j in range(4):
                    if j > 0:
                        dve.wait_ge(S("du"), 4 * h + j + 1)
                        scan_step(j, 0, 0)
                        scan_step(j, 0, 1)
                        gate(j - 1)
                    if j == 1:
                        delta(3)
                    with dve.Fori(1, N2) as n2:
                        scan_step(j, n2, 0)
                        scan_step(j, n2, 1)
                gate(3)
                center(0, h, 1)
                variance(0, h, 1)
                center(1, h, 1)
                variance(1, h, 1)
                normalize(0, h, 1)
                normalize(1, h, 1)
                def add_block(k):
                    dve.wait_ge(S("proj"), 2 * h + k + 1)
                    stt(D[k]["X3"].rearrange("p (w h) -> p h w", w=W), img(PS[2 * k]), vc("proj_b"), img(D[k]["X2"]), ALU.add, ALU.add).then_inc(S("X3"), 1)

                def x3_stats(k):
                    dve.wait_ge(S("X3"), 2 * h + k + 1)
                    stats(D[k]["X3"], D[k], h, 3, k)

                add_block(0)
                x3_stats(0)
                add_block(1)
                group_var(D[0], h, 3, 0)
                x3_stats(1)
                group_shift(D[0], h, 3, 0)
                group_norm(D[1], h, 3, 1)


def kernel(**inputs):
    import numpy as np
    import concourse.bacc as bacc
    from concourse.bass_utils import run_bass_kernel_spmd

    v = {k: np.asarray(a) for k, a in inputs.items()}

    def two(a):
        return np.concatenate([a, a], axis=0)

    cols = []
    for n in VEC:
        if n[0] in "go" and n != "skip":
            cols.append(two(v["L0_conv_" + n]))
        elif n == "conv_bias":
            cols.append(two(v["L1_conv_bias"]))
        elif n in ("ln_g", "ln_b", "proj_b"):
            cols.append(two(v["L2_conv_" + n]))
        elif n == "m_conv_b":
            cols.append(v["L2_conv_conv_b"])
        elif n == "m_dt_b":
            cols.append(v["L2_conv_dt_proj_b"])
        elif n == "m_D":
            cols.append(v["L2_conv_D"])
        else:
            cols.append(np.broadcast_to(v["L2_conv_skip_scale"], (P,)))
    wg = v["L0_conv_wg"].reshape(9, C).T
    wg1 = v["L0_conv_wg1"].reshape(9, C).T
    row32 = np.zeros((P, 32), np.float32)
    row32[np.arange(P), np.arange(P) % 32] = 1.0
    vec = np.concatenate([np.stack(cols, axis=1), two(wg), two(wg1), v["L2_conv_conv_w"], v["L2_conv_A_log"], row32], axis=1)

    r = np.arange(P)
    eye = np.eye(P, dtype=np.float32)
    group = (r[:, None] // 2 == r[None, :] // 2).astype(np.float32) * np.float32(0.5)
    prev = (r // C) * C + (r % C - 1) % C
    nxt = (r // C) * C + (r % C + 1) % C
    up = np.zeros((P, P), np.float32)
    up[prev, r] = 1.0
    down = np.zeros((P, P), np.float32)
    down[nxt, r] = 1.0
    n = np.arange(H)
    m = np.cos(np.pi * (n[None, :] + 0.5) * n[:, None] / H) * np.sqrt(2.0 / H)
    m[0] *= 1.0 / np.sqrt(2.0)
    dct = np.zeros((P, P), np.float32)
    for q in range(4):
        dct[q * H:(q + 1) * H, q * H:(q + 1) * H] = m.T
    mats = np.concatenate([eye, -eye, group, up, down, down - up, dct], axis=1).astype(np.float32)

    conv = v["L1_conv_kernel"].reshape(9, C, C)
    conv_w = np.zeros((P, 9, P), np.float32)
    proj_w = np.zeros((P, P), np.float32)
    in_w = np.zeros((P, 2, 2 * P), np.float32)
    for b in range(2):
        s = slice(b * C, b * C + C)
        conv_w[s, :, s] = conv.transpose(1, 0, 2)
        proj_w[s, s] = v["L2_conv_proj_w"].T
        in_w[s, b] = v["L2_conv_in_proj_w"].T
    xw = v["L2_conv_x_proj_w"]
    xbc_w = np.concatenate([xw[4:].T] * 3, axis=1)

    arrays = {"x": v["x"], "vec": vec, "mats": mats, "conv_w": conv_w.reshape(P, 9 * P), "in_w": in_w.reshape(P, 4 * P),
              "xbc_w": xbc_w, "xdt_w": xw[:4], "dtp_w": v["L2_conv_dt_proj_w"].T,
              "out_w": v["L2_conv_out_proj_w"].T, "proj_w": proj_w}
    arrays = {k: np.ascontiguousarray(a) for k, a in arrays.items()}

    nc = bacc.Bacc("TRN2", target_bir_lowering=False, num_devices=1)
    args = [nc.dram_tensor(k, a.shape, mybir.dt.from_np(a.dtype), kind="ExternalInput").ap() for k, a in arrays.items()]
    out = nc.dram_tensor("out", (B, H, W, C), fp32, kind="ExternalOutput").ap()
    fused_blocks(nc, *args, out)
    res = run_bass_kernel_spmd(nc, [arrays], core_ids=[0])
    return res.results[0]["out"]
```
